# Optimizing a Trainium2 kernel written in Bass

```python
import numpy as np
import jax
import jax.numpy as jnp

def _softmax(x, axis=-1):
    return jax.nn.softmax(x, axis=axis)

def _gelu(x):
    return jax.nn.gelu(x, approximate=True)

def _silu(x):
    return jax.nn.silu(x)

def _sigmoid(x):
    return jax.nn.sigmoid(x)

def _layernorm(x, axis=-1, eps=1e-05):
    m = jnp.mean(x, axis=axis, keepdims=True)
    v = jnp.var(x, axis=axis, keepdims=True)
    return (x - m) / jnp.sqrt(v + eps)

def _scatter_add(tgt, idx, src, axis=0):
    return tgt.at[idx].add(src)

def _segment_sum(src, seg, n):
    return jax.ops.segment_sum(src, seg, n)
kernel_name = 'mk_audio_tower_d1_tok_audfeat1024_r4_018d99'

def setup_inputs(seed: int=0):
    np.random.seed(seed)
    _w = jnp.asarray

    def _rec_inputs():
        import jax
        import jax.numpy as jnp
        _rk = jax.random.key(seed)
        x = -0.000125008 + 0.999885 * jax.random.normal(jax.random.fold_in(_rk, 1), (64, 125, 64), jnp.float32)
        return x
    x = _rec_inputs()

    def _L0_tok_setup():
        import jax, jax.numpy as jnp
        import numpy as np
        from jax import lax
        N_CHANNELS = 64
        FRONTEND_DIM = 256
        TEMPORAL_KERNEL = 32
        TEMPORAL_STRIDE = 4
        GAUSS_SIGMA = 2.0
        GAUSS_KSIZE = int(GAUSS_SIGMA * 4) + 1
        GAUSS_PAD = GAUSS_KSIZE // 2
        LN_EPS = 1e-05

        def _gaussian_kernel():
            t = jnp.arange(GAUSS_KSIZE, dtype=jnp.float32) - (GAUSS_KSIZE - 1) / 2
            g = jnp.exp(-t ** 2 / (2.0 * GAUSS_SIGMA ** 2))
            return g / g.sum()

        def _depthwise_conv1d(x_nct, w_c1k, stride, pad):
            return lax.conv_general_dilated(x_nct, w_c1k, window_strides=(stride,), padding=[(pad, pad)], dimension_numbers=('NCH', 'OIH', 'NCH'), feature_group_count=N_CHANNELS)
        key = jax.random.key(seed)
        k1, k2, k3, k4, k5, k6 = jax.random.split(key, 6)
        B, T, C, D = (16, 2048, N_CHANNELS, FRONTEND_DIM)
        x = jax.random.normal(k1, (B, T, C), dtype=jnp.float32)
        w_temporal = jax.random.normal(k2, (C, 1, TEMPORAL_KERNEL), dtype=jnp.float32) * (1.0 / TEMPORAL_KERNEL)
        w_proj = jax.random.normal(k3, (D, C), dtype=jnp.float32) * (1.0 / np.sqrt(C))
        b_proj = jax.random.normal(k4, (D,), dtype=jnp.float32) * 0.01
        ln_gamma = jnp.ones((D,), dtype=jnp.float32)
        ln_beta = jnp.zeros((D,), dtype=jnp.float32)
        return {'x': x, 'w_temporal': w_temporal, 'w_proj': w_proj, 'b_proj': b_proj, 'ln_gamma': ln_gamma, 'ln_beta': ln_beta}
    _L0_tok_all = _L0_tok_setup()
    _L0_tok_in = {k: v for k, v in _L0_tok_all.items() if k in ('w_temporal', 'w_proj', 'b_proj', 'ln_gamma', 'ln_beta')}
    del _L0_tok_all

    def _L0_attn_setup():
        import jax, jax.numpy as jnp
        import numpy as np
        key = jax.random.key(seed)
        k1, k2, k3 = jax.random.split(key, 3)
        B, S, D, N = (2, 512, 256, 16)
        H = D // N
        x = jax.random.normal(k1, (B, S, D), dtype=jnp.float32)
        W_qkv = jax.random.normal(k2, (N, D, 3 * H), dtype=jnp.float32) / np.sqrt(D).astype(np.float32)
        W_out = jax.random.normal(k3, (N, H, D), dtype=jnp.float32) / np.sqrt(D).astype(np.float32)
        return {'x': x, 'W_qkv': W_qkv, 'W_out': W_out}
    _L0_attn_all = _L0_attn_setup()
    _L0_attn_in = {k: v for k, v in _L0_attn_all.items() if k in ('W_qkv', 'W_out')}
    del _L0_attn_all

    def _L0_ffn_setup():
        import jax, jax.numpy as jnp
        import numpy as np
        B, N, D, E, R, K = (4, 512, 256, 8, 64, 2)
        key = jax.random.key(seed)
        ks = jax.random.split(key, 5)
        scale = 0.02
        return {'x': jax.random.normal(ks[0], (B, N, D), dtype=jnp.float32), 'gate_w': jax.random.normal(ks[1], (D, E), dtype=jnp.float32) * scale, 'Wu': jax.random.normal(ks[2], (E, D, R), dtype=jnp.float32) * scale, 'Wv': jax.random.normal(ks[3], (E, D, R), dtype=jnp.float32) * scale, 'Wo': jax.random.normal(ks[4], (E, R, D), dtype=jnp.float32) * scale}
    _L0_ffn_all = _L0_ffn_setup()
    _L0_ffn_in = {k: v for k, v in _L0_ffn_all.items() if k in ('gate_w', 'Wu', 'Wv', 'Wo')}
    del _L0_ffn_all
    return {'x': x, 'L0_tok_w_temporal': _L0_tok_in['w_temporal'], 'L0_tok_w_proj': _L0_tok_in['w_proj'], 'L0_tok_b_proj': _L0_tok_in['b_proj'], 'L0_tok_ln_gamma': _L0_tok_in['ln_gamma'], 'L0_tok_ln_beta': _L0_tok_in['ln_beta'], 'L0_attn_W_qkv': _L0_attn_in['W_qkv'], 'L0_attn_W_out': _L0_attn_in['W_out'], 'L0_ffn_gate_w': _L0_ffn_in['gate_w'], 'L0_ffn_Wu': _L0_ffn_in['Wu'], 'L0_ffn_Wv': _L0_ffn_in['Wv'], 'L0_ffn_Wo': _L0_ffn_in['Wo']}

def reference(x, L0_tok_w_temporal, L0_tok_w_proj, L0_tok_b_proj, L0_tok_ln_gamma, L0_tok_ln_beta, L0_attn_W_qkv, L0_attn_W_out, L0_ffn_gate_w, L0_ffn_Wu, L0_ffn_Wv, L0_ffn_Wo):
    import jax
    import jax.numpy as jnp

    def _L0_tok_ref(x, w_temporal, w_proj, b_proj, ln_gamma, ln_beta):
        import jax, jax.numpy as jnp
        import numpy as np
        from jax import lax
        N_CHANNELS = 64
        FRONTEND_DIM = 256
        TEMPORAL_KERNEL = 32
        TEMPORAL_STRIDE = 4
        GAUSS_SIGMA = 2.0
        GAUSS_KSIZE = int(GAUSS_SIGMA * 4) + 1
        GAUSS_PAD = GAUSS_KSIZE // 2
        LN_EPS = 1e-05

        def _gaussian_kernel():
            t = jnp.arange(GAUSS_KSIZE, dtype=jnp.float32) - (GAUSS_KSIZE - 1) / 2
            g = jnp.exp(-t ** 2 / (2.0 * GAUSS_SIGMA ** 2))
            return g / g.sum()

        def _depthwise_conv1d(x_nct, w_c1k, stride, pad):
            return lax.conv_general_dilated(x_nct, w_c1k, window_strides=(stride,), padding=[(pad, pad)], dimension_numbers=('NCH', 'OIH', 'NCH'), feature_group_count=N_CHANNELS)
        x_nct = jnp.transpose(x, (0, 2, 1))
        gk = jnp.broadcast_to(_gaussian_kernel()[None, None, :], (N_CHANNELS, 1, GAUSS_KSIZE))
        x_smooth = _depthwise_conv1d(x_nct, gk, stride=1, pad=GAUSS_PAD)
        x_strided = _depthwise_conv1d(x_smooth, w_temporal, stride=TEMPORAL_STRIDE, pad=0)
        x_strided = jnp.transpose(x_strided, (0, 2, 1))
        h = jnp.einsum('btc,dc->btd', x_strided, w_proj) + b_proj
        mu = jnp.mean(h, axis=-1, keepdims=True)
        xc = h - mu
        var = jnp.mean(xc * xc, axis=-1, keepdims=True)
        out = xc * lax.rsqrt(var + LN_EPS) * ln_gamma + ln_beta
        return out

    def _L0_attn_ref(x, W_qkv, W_out):
        import jax, jax.numpy as jnp
        import numpy as np
        B, S, D = x.shape
        head_dim = W_qkv.shape[-1] // 3
        qkv = jnp.einsum('bsd,ndh->bnsh', x, W_qkv)
        q, k, v = jnp.split(qkv, 3, axis=-1)
        scale = jnp.asarray(1.0 / np.sqrt(head_dim), dtype=x.dtype)
        attn = jnp.einsum('bnqh,bnkh->bnqk', q, k) * scale
        mask = jnp.asarray(-10000000000.0, dtype=x.dtype) * (1.0 - jnp.tril(jnp.ones((S, S), dtype=x.dtype)))
        attn = jax.nn.softmax(attn + mask, axis=-1)
        out = jnp.einsum('bnqk,bnkh->bnqh', attn, v)
        out = out.reshape(B, -1, S)
        return jnp.einsum('bds,nhd->bsd', out, W_out)

    def _L0_ffn_ref(x, gate_w, Wu, Wv, Wo):
        import jax, jax.numpy as jnp
        import numpy as np
        B, N, D, E, R, K = (4, 512, 256, 8, 64, 2)
        logits = jnp.einsum('bnd,de->bne', x, gate_w)
        topv, topi = jax.lax.top_k(logits, K)
        w = jax.nn.softmax(topv, axis=-1)
        u = jnp.einsum('bnd,edr->bner', x, Wu)
        v = jnp.einsum('bnd,edr->bner', x, Wv)
        s = jax.nn.silu(u) * v
        Y = jnp.einsum('bner,erd->bned', s, Wo)
        y_sel = jnp.take_along_axis(Y, topi[..., None], axis=2)
        out = jnp.einsum('bnkd,bnk->bnd', y_sel, w)
        return out
    h = _L0_tok_ref(x, L0_tok_w_temporal, L0_tok_w_proj, L0_tok_b_proj, L0_tok_ln_gamma, L0_tok_ln_beta)
    h = h + _L0_attn_ref(_layernorm(h, axis=-1), L0_attn_W_qkv, L0_attn_W_out)
    h = h + _L0_ffn_ref(_layernorm(h, axis=-1), L0_ffn_gate_w, L0_ffn_Wu, L0_ffn_Wv, L0_ffn_Wo)
    return h

_drawn_inputs = setup_inputs


def setup_inputs(seed=0):
    import zlib

    import numpy as np

    out = dict(_drawn_inputs(seed))
    spreads = {'L0_tok_ln_gamma': (1.0, 0.2), 'L0_tok_ln_beta': (0.0, 0.1)}
    factors = {'L0_ffn_gate_w': 8.0, 'L0_ffn_Wu': 8.0, 'L0_ffn_Wv': 8.0, 'L0_ffn_Wo': 8.0}
    for name, (base, spread) in spreads.items():
        noise = np.random.default_rng([zlib.crc32(name.encode()), seed]).standard_normal(out[name].shape)
        drawn = base * np.exp(spread * noise) if base else spread * noise
        out[name] = jnp.asarray(drawn.astype(out[name].dtype))
    for name, factor in factors.items():
        out[name] = (out[name] * factor).astype(out[name].dtype)
    return out
```

```python
from contextlib import ExitStack

import concourse.bass as bass
from concourse import mybir

B, T, C = 64, 125, 64
S, D = 24, 256
NH, HD = 16, 16
E, R = 8, 64
TAPS, STRIDE, GPAD = 32, 4, 4
EPS = 1e-5
G = 4
BG = B // G
TOK = BG * S
NJ = TOK // 128
SG = S // NJ
Q4 = BG // 4
NF = E * R // 128
NP = 4 + NJ
SPAN = STRIDE * (S - 1)
PAD = 8

F32 = mybir.dt.float32
BF16 = mybir.dt.bfloat16
U32 = mybir.dt.uint32
ALU = mybir.AluOpType
ACT = mybir.ActivationFunctionType
X = mybir.AxisListType.X


def build(nc, x_in, band_in, taps_in, wproj_in, gamma_in, beta_in, wqkv_in, wout_in, gate_in, wup_in, wdown_in,
          constf_in, constb_in, out, v_scratch, o_scratch):
    with ExitStack() as ctx:
        def sb(name, shape, dt=F32):
            return ctx.enter_context(nc.sbuf_tensor(name, shape, dt))

        def sem(name):
            return ctx.enter_context(nc.semaphore(name))

        bank = [ctx.enter_context(nc.psum_tensor(f"bank{i}", [128, 512], F32)) for i in range(8)]

        x_sb = sb("x_sb", [T, C, B])
        band = sb("band", [TAPS, T + SPAN])
        taps = sb("taps", [TAPS, C])
        wproj = sb("wproj", [C + 1, D])
        gamma = sb("gamma", [128, D])
        beta = sb("beta", [128, D])
        wqkv = sb("wqkv", [128, 2, 3 * D])
        wout = sb("wout", [128, 2, D])
        gate = sb("gate", [128, 2, E])
        wup = sb("wup", [128, 2, 2 * E * R])
        wdown = sb("wdown", [128, NF, D])
        constf = sb("constf", [128, 144])
        constb = sb("constb", [128, 128 + NH * S], BF16)
        ident = constf[:, 0:128]
        headsel = constf[:, 128:136]
        iota = constf[:, 136:144]
        identb = constb[:, 0:128]
        causal = constb[:, 128:128 + NH * S]
        ones = sb("ones", [128, 128])
        neghalf = sb("neghalf", [128, NJ])

        toep = sb("toep", [T, C, S])
        y_b = sb("y_b", [B, C, S])
        yT = sb("yT", [C + 1, S, B])
        wsum = sb("wsum", [128, D])
        y_stage = sb("y_stage", [C + 1, NJ, SG, BG])
        h_raw = sb("h_raw", [128, NJ, D])
        hres = sb("hres", [128, G * NJ, D])
        z1 = sb("z1", [128, NJ, D])
        zT = sb("zT", [128, 2, TOK])
        stats = [sb(f"stats{i}", [128, NJ, 6]) for i in range(3)]
        meanvar = [sb(f"meanvar{i}", [128, NJ, 2]) for i in range(3)]
        vareps = [sb(f"vareps{i}", [128, NJ]) for i in range(3)]
        rstd = [sb(f"rstd{i}", [128, NJ]) for i in range(3)]

        kT = sb("kT", [128, 2, TOK])
        kexp = sb("kexp", [128, 2, 8, TOK])
        qT = sb("qT", [128, 2, TOK + PAD])
        v_sb = sb("v_sb", [128, NJ, D])
        vdiag = sb("vdiag", [4 * S, BG, 4, 4, HD])
        smax = sb("smax", [128, Q4, NH])
        probs = sb("probs", [128, Q4, NH * S])
        ssum = sb("ssum", [128, Q4, NH])
        rsum = sb("rsum", [128, Q4, NH])
        pT = sb("pT", [4 * S, Q4, 4, 128])
        o_sb = sb("o_sb", [128, Q4, HD, NH])

        r_sb = sb("r_sb", [128, D // NH, NJ, NH])
        rw = sb("rw", [128, NJ, D])
        z2 = sb("z2", [128, NJ, D])
        z2T = sb("z2T", [128, 2, TOK])
        logitT = sb("logitT", [E, TOK])
        logits = sb("logits", [128, NJ, E])
        top = sb("top", [128, NJ, 8])
        topi = sb("topi", [128, NJ, 8], U32)
        topf = sb("topf", [128, NJ, 8])
        gap = sb("gap", [128, NJ])
        egap = sb("egap", [128, NJ])
        egap1 = sb("egap1", [128, NJ])
        w_first = sb("w_first", [128, NJ])
        w_second = sb("w_second", [128, NJ])
        wa = sb("wa", [128, NJ, E])
        wb = sb("wb", [128, NJ, E])
        wt = sb("wt", [128, NJ, E])
        wexp = sb("wexp", [128, NJ, E, R])
        th = sb("th", [128, 2, TOK])
        ug = sb("ug", [128, 2, TOK])
        sT = sb("sT", [128, NF, TOK])
        out_sb = sb("out_sb", [128, NJ, D])

        ld_small = sem("ld_small")
        ld_x = [sem(f"ld_x{i}") for i in range(4)]
        ld_const = sem("ld_const")
        ld_front = sem("ld_front")
        ld_qkv = sem("ld_qkv")
        ld_ffn = sem("ld_ffn")
        v_stored = sem("v_stored")
        v_loaded = sem("v_loaded")
        o_stored = sem("o_stored")
        r_loaded = sem("r_loaded")
        out_stored = sem("out_stored")
        pe_toep, pe_conv, pe_yT, pe_wsum = sem("pe_toep"), sem("pe_conv"), sem("pe_yT"), sem("pe_wsum")
        pe_proj, pe_h, pe_zT = sem("pe_proj"), sem("pe_h"), sem("pe_zT")
        pe_z2T, pe_logit, pe_logits = sem("pe_z2T"), sem("pe_logit"), sem("pe_logits")
        pe_up, pe_score, pe_wbc = sem("pe_up"), sem("pe_score"), sem("pe_wbc")
        pe_pT, pe_o, pe_y = sem("pe_pT"), sem("pe_o"), sem("pe_y")
        act_toep, act_yb, act_yT, act_wsum = sem("act_toep"), sem("act_yb"), sem("act_yT"), sem("act_wsum")
        act_proj, act_h, act_zT = sem("act_proj"), sem("act_h"), sem("act_zT")
        act_z2T, act_logit, act_egap = sem("act_z2T"), sem("act_logit"), sem("act_egap")
        act_tanh, act_exp, act_pT = sem("act_tanh"), sem("act_exp"), sem("act_pT")
        dve_ones = sem("dve_ones")
        dve_toep, dve_yb = sem("dve_toep"), sem("dve_yb")
        dve_stats = [sem(f"dve_stats{i}") for i in range(3)]
        dve_mv = [sem(f"dve_mv{i}") for i in range(3)]
        dve_xn, dve_z1, dve_rw, dve_h2, dve_z2 = sem("dve_xn"), sem("dve_z1"), sem("dve_rw"), sem("dve_h2"), sem("dve_z2")
        dve_logits, dve_top, dve_topi, dve_topf = sem("dve_logits"), sem("dve_top"), sem("dve_topi"), sem("dve_topf")
        dve_gap, dve_e1, dve_w1, dve_w2 = sem("dve_gap"), sem("dve_e1"), sem("dve_w1"), sem("dve_w2")
        dve_wab, dve_wt = sem("dve_wab"), sem("dve_wt")
        dve_up, dve_s = sem("dve_up"), sem("dve_s")
        dve_max, dve_sub, dve_sum, dve_rsum, dve_o, dve_y = (
            sem("dve_max"), sem("dve_sub"), sem("dve_sum"), sem("dve_rsum"), sem("dve_o"), sem("dve_y"))
        pool_zero, pool_ys, pool_kexp = sem("pool_zero"), sem("pool_ys"), sem("pool_kexp")
        pool_gamma, pool_h1, pool_wexp = sem("pool_gamma"), sem("pool_h1"), sem("pool_wexp")
        pool_var = [sem(f"pool_var{i}") for i in range(3)]
        pool_rstd = [sem(f"pool_rstd{i}") for i in range(3)]
        N_ZERO = 3

        block = ctx.enter_context(nc.Block())

        @block.sync
        def _(sp):
            sp.dma_start(band[:, :], band_in).then_inc(ld_small, 16)
            sp.dma_start(taps[:, :], taps_in).then_inc(ld_small, 16)
            for i in range(4):
                q = C // 4
                sp.dma_start(x_sb[:, i * q:(i + 1) * q, :], x_in[:, i * q:(i + 1) * q, :]).then_inc(ld_x[i], 16)
            sp.dma_start(wup[:, :, :], wup_in.rearrange("(c p) n -> p c n", p=128)).then_inc(ld_ffn, 16)
            sp.dma_start(wdown[:, :, :], wdown_in.rearrange("(c p) n -> p c n", p=128)).then_inc(ld_ffn, 16)
            sp.dma_start(gate[:, :, :], gate_in.rearrange("(c p) n -> p c n", p=128)).then_inc(ld_ffn, 16)

            def attend(g):
                sp.wait_ge(act_proj, NP * (g + 1))
                if g >= 1:
                    sp.wait_ge(v_loaded, 64 * g)
                sp.dma_start(v_scratch.rearrange("j p d -> p j d"), v_sb[:, :, :]).then_inc(v_stored, 16)
                sp.wait_ge(v_stored, 16 * (g + 1))
                sp.wait_ge(pool_zero, N_ZERO)
                if g >= 1:
                    sp.wait_ge(pe_o, Q4 * g)
                rows = v_scratch.rearrange("j p d -> (j p) d").rearrange("(b k) (n c) -> k b n c", k=S, n=4)
                for n in range(4):
                    sp.dma_start(vdiag[n * S:(n + 1) * S, :, n, :, :].rearrange("k b g h -> k b (g h)"),
                                 rows[:, :, n, :]).then_inc(v_loaded, 16)
                for u in range(Q4):
                    sp.wait_ge(dve_o, Q4 * g + u + 1)
                    if g >= 1 and u == 0:
                        sp.wait_ge(r_loaded, 16 * SG * g)
                    sp.dma_start(o_scratch[u], o_sb[:, u, :, :].rearrange("p h n -> p (h n)")).then_inc(o_stored, 16)
                sp.wait_ge(o_stored, 64 * (g + 1))
                if g >= 1:
                    sp.wait_ge(dve_rw, g)
                for k in range(SG):
                    src = bass.AP(tensor=o_scratch.tensor, offset=o_scratch.offset + k * NJ * NH,
                                  ap=[[32 * D, BG], [S * NH, D // NH], [1, NJ * NH]])
                    sp.dma_start(r_sb[k * BG:(k + 1) * BG, :, :, :].rearrange("p d j n -> p d (j n)"), src
                                 ).then_inc(r_loaded, 16)

            def store(c):
                sp.wait_ge(dve_y, NJ * (c + 1))
                dst = out[c * BG:(c + 1) * BG].rearrange("b (s j) d -> s b (j d)", j=NJ)
                sp.dma_start(dst, out_sb[:, :, :].rearrange("p j d -> p (j d)")).then_inc(out_stored, 16)

            for i in range(G + 1):
                if i < G:
                    attend(i)
                if i >= 1:
                    store(i - 1)
            sp.wait_ge(out_stored, 16 * G)

        @block.gpsimd
        def _(pool):
            pool.memset(vdiag[:, :, :, :, :], 0.0).then_inc(pool_zero, 1)
            pool.memset(qT[:, :, TOK:TOK + PAD], 0.0).then_inc(pool_zero, 1)
            pool.memset(neghalf[:, :], -0.5).then_inc(pool_zero, 1)
            pool.wait_ge(pool_zero, N_ZERO)
            pool.wait_ge(ld_const, 32)
            pool.wait_ge(ld_front, 80)
            pool.wait_ge(act_yT, 3)

            def rsqrt(k, n):
                pool.wait_ge(dve_mv[k], NJ * (n + 1))
                pool.tensor_scalar(vareps[k][:, :], meanvar[k][:, :, 1], EPS, None, ALU.add).then_inc(pool_var[k], 1)
                pool.wait_ge(pool_var[k], n + 1)
                pool.tensor_tensor(rstd[k][:, :], vareps[k][:, :], neghalf[:, :], ALU.pow).then_inc(pool_rstd[k], 1)

            def stage_y(n):
                if n >= 1:
                    pool.wait_ge(pe_h, NJ * n)
                pool.tensor_copy(y_stage[:, :, :, :],
                                 yT[:, :, n * BG:(n + 1) * BG].rearrange("c (s j) b -> c j s b", j=NJ)
                                 ).then_inc(pool_ys, 1)

            def front(n):
                rsqrt(0, n)
                pool.wait_ge(dve_xn, NJ * (n + 1))
                h1 = hres[:, NJ * n:NJ * n + NJ, :]
                pool.tensor_tensor(h1, h1, gamma[:, :].unsqueeze(1).to_broadcast([128, NJ, D]), ALU.mult
                                   ).then_inc(pool_gamma, 1)
                pool.wait_ge(pool_gamma, n + 1)
                pool.tensor_tensor(h1, h1, beta[:, :].unsqueeze(1).to_broadcast([128, NJ, D]), ALU.add
                                   ).then_inc(pool_h1, 1)
                rsqrt(1, n)

            def expand_keys(g, half):
                pool.wait_ge(act_proj, NP * g + half + 1)
                if g >= 1 and half == 0:
                    pool.wait_ge(pe_score, Q4 * g)
                for n in range(8):
                    pool.tensor_scalar(kexp[:, half, n, :], kT[:, half, :], headsel[:, n:n + 1], None, ALU.mult
                                       ).then_inc(pool_kexp, 1)

            def expand_weights(c):
                pool.wait_ge(dve_wt, c + 1)
                if c >= 1:
                    pool.wait_ge(pe_wbc, NF * c)
                pool.tensor_copy(wexp[:, :, :, :], wt[:, :, :].unsqueeze(3).to_broadcast([128, NJ, E, R])
                                 ).then_inc(pool_wexp, 1)

            stage_y(0)
            front(0)
            for i in range(G + 1):
                if i + 1 < G:
                    stage_y(i + 1)
                if i < G:
                    expand_keys(i, 0)
                if i >= 1:
                    rsqrt(2, i - 1)
                if i < G:
                    expand_keys(i, 1)
                if i >= 1:
                    expand_weights(i - 1)
                if i + 1 < G:
                    front(i + 1)

        @block.scalar
        def _(act):
            act.dma_start(constf[:, :], constf_in).then_inc(ld_const, 16)
            act.dma_start(constb[:, :], constb_in).then_inc(ld_const, 16)
            act.dma_start(wproj[:, :], wproj_in).then_inc(ld_front, 16)
            act.dma_start(gamma[:, :], gamma_in.partition_broadcast(128)).then_inc(ld_front, 16)
            act.dma_start(beta[:, :], beta_in.partition_broadcast(128)).then_inc(ld_front, 16)
            act.dma_start(wout[:, :, :], wout_in.rearrange("(c p) n -> p c n", p=128)).then_inc(ld_front, 32)
            act.dma_start(wqkv[:, :, :], wqkv_in.rearrange("(c p) n -> p c n", p=128)).then_inc(ld_qkv, 16)

            for k in range(3):
                act.wait_ge(pe_toep, k + 1)
                act.copy(toep[:, :, 8 * k:8 * k + 8], bank[k][0:T, :].rearrange("p (t c) -> p c t", t=8)
                         ).then_inc(act_toep, 1)
            for k in range(4):
                act.wait_ge(pe_conv, k + 1)
                act.copy(y_b[:, 16 * k:16 * k + 16, :], bank[3 + k][0:B, 0:16 * S].rearrange("p (c t) -> p c t", t=S)
                         ).then_inc(act_yb, 1)
            act.wait_ge(dve_ones, 2)
            for k in range(3):
                act.wait_ge(pe_yT, k + 1)
                act.copy(yT[0:C, 8 * k:8 * k + 8, :], bank[k][0:C, :].rearrange("p (t b) -> p t b", t=8)
                         ).then_inc(act_yT, 1)
            act.wait_ge(pe_wsum, 1)
            act.copy(wsum[:, :], bank[7][:, 0:D]).then_inc(act_wsum, 1)

            def project(g):
                for k in range(NP):
                    act.wait_ge(pe_proj, NP * g + k + 1)
                    p = bank[k % 2]
                    if k < 2:
                        if g >= 1:
                            act.wait_ge(pool_kexp, 16 * g)
                        ins = act.copy(kT[:, k, :], p[:, 0:TOK])
                    elif k < 4:
                        if g >= 1:
                            act.wait_ge(pe_score, Q4 * g)
                        ins = act.mul(qT[:, k - 2, 0:TOK], p[:, 0:TOK], HD ** -0.5)
                    else:
                        if g >= 1:
                            act.wait_ge(v_stored, 16 * g)
                        ins = act.copy(v_sb[:, k - 4, :], p[:, 0:D])
                    ins.then_inc(act_proj, 1)

            def front_h(n):
                for j in range(NJ):
                    act.wait_ge(pe_h, NJ * n + j + 1)
                    if n >= 1:
                        act.wait_ge(dve_xn, NJ * n)
                    act.copy(h_raw[:, j, :], bank[6 + j % 2][:, 0:D]).then_inc(act_h, 1)

            def front_zT(n):
                if n >= 1:
                    act.wait_ge(pe_proj, NP * n)
                for k in range(2):
                    act.wait_ge(pe_zT, 2 * n + k + 1)
                    act.copy(zT[:, k, 0:TOK].rearrange("p (b s j) -> p j s b", b=BG, j=NJ),
                             bank[6 + k][:, 0:TOK].rearrange("p (j s b) -> p j s b", j=NJ, s=SG)
                             ).then_inc(act_zT, 1)

            def feed_z2T(c):
                for k in range(2):
                    act.wait_ge(pe_z2T, 2 * c + k + 1)
                    if c >= 1:
                        act.wait_ge(pe_up, 8 * c)
                    act.copy(z2T[:, k, :], bank[7 - k][:, 0:TOK]).then_inc(act_z2T, 1)
                act.wait_ge(pe_logit, c + 1)
                act.copy(logitT[:, :], bank[7][0:E, 0:TOK]).then_inc(act_logit, 1)

            def tanh(c, j):
                act.wait_ge(pe_up, 8 * c + 2 * j + 1)
                if j >= 2:
                    act.wait_ge(dve_up, 8 * c + 2 * j - 3)
                act.activation(th[:, j % 2, :], bank[0][:, 0:TOK], ACT.Tanh, scale=0.5).then_inc(act_tanh, 1)

            def exp_gap(c):
                act.wait_ge(dve_gap, c + 1)
                act.activation(egap[:, :], gap[:, :], ACT.Exp).then_inc(act_egap, 1)

            def exp_scores(g):
                for u in range(Q4):
                    act.wait_ge(dve_sub, Q4 * g + u + 1)
                    act.activation(probs[:, u, :], probs[:, u, :], ACT.Exp).then_inc(act_exp, 1)

            def evac_pT(g):
                for u in range(Q4):
                    act.wait_ge(pe_pT, Q4 * g + u + 1)
                    if g >= 1 and u == 0:
                        act.wait_ge(pe_o, Q4 * g)
                    act.copy(pT[:, u, :, :], bank[4 + u % 2][0:4 * S, :].rearrange("p (n q) -> p n q", n=4)
                             ).then_inc(act_pT, 1)

            front_h(0)
            front_zT(0)
            for i in range(G + 1):
                if i < G:
                    project(i)
                if i + 1 < G:
                    front_h(i + 1)
                if i >= 1:
                    feed_z2T(i - 1)
                    tanh(i - 1, 0)
                    tanh(i - 1, 1)
                    exp_gap(i - 1)
                if i < G:
                    exp_scores(i)
                if i >= 1:
                    tanh(i - 1, 2)
                    tanh(i - 1, 3)
                if i < G:
                    evac_pT(i)
                if i + 1 < G:
                    front_zT(i + 1)

        @block.vector
        def _(dve):
            dve.memset(ones[:, :], 1.0).then_inc(dve_ones, 1)
            dve.memset(yT[C:C + 1, :, :], 1.0).then_inc(dve_ones, 1)

            def layer_stats(k, n, src):
                for j in range(NJ):
                    dve.bn_stats(stats[k][:, j, :], src(j)).then_inc(dve_stats[k], 1)
                for j in range(NJ):
                    dve.wait_ge(dve_stats[k], NJ * n + j + 1)
                    dve.bn_aggr(meanvar[k][:, j, :], stats[k][:, j, :]).then_inc(dve_mv[k], 1)

            def normalise(k, n, dst, src, done):
                dve.wait_ge(pool_rstd[k], n + 1)
                for j in range(NJ):
                    dve.tensor_scalar(dst(j), src(j), meanvar[k][:, j, 0:1], rstd[k][:, j:j + 1],
                                      ALU.subtract, ALU.mult).then_inc(done, 1)

            def front_stats(n):
                dve.wait_ge(act_h, NJ * (n + 1))
                layer_stats(0, n, lambda j: h_raw[:, j, :])

            def front_norm(n):
                normalise(0, n, lambda j: hres[:, NJ * n + j, :], lambda j: h_raw[:, j, :], dve_xn)

            def front_stats2(n):
                dve.wait_ge(pool_h1, n + 1)
                layer_stats(1, n, lambda j: hres[:, NJ * n + j, :])

            def front_norm2(n):
                if n >= 1:
                    dve.wait_ge(pe_zT, 2 * n)
                normalise(1, n, lambda j: z1[:, j, :], lambda j: hres[:, NJ * n + j, :], dve_z1)

            def feed_residual(c):
                dve.wait_ge(r_loaded, 16 * SG * (c + 1))
                dve.tensor_tensor(rw[:, :, :].rearrange("p j (n d) -> p j n d", n=NH),
                                  r_sb[:, :, :, :].rearrange("p d j n -> p j n d"),
                                  wsum[:, :].rearrange("p (n d) -> p n d", n=NH).unsqueeze(1)
                                  .to_broadcast([128, NJ, NH, D // NH]), ALU.mult).then_inc(dve_rw, 1)
                dve.wait_ge(dve_rw, c + 1)
                h = hres[:, NJ * c:NJ * c + NJ, :]
                dve.tensor_tensor(h, h, rw[:, :, :], ALU.add).then_inc(dve_h2, 1)
                dve.wait_ge(dve_h2, c + 1)
                layer_stats(2, c, lambda j: hres[:, NJ * c + j, :])
                if c >= 1:
                    dve.wait_ge(pe_z2T, 2 * c)
                normalise(2, c, lambda j: z2[:, j, :], lambda j: hres[:, NJ * c + j, :], dve_z2)

            def feed_gate(c):
                dve.wait_ge(pe_logits, c + 1)
                dve.tensor_copy(logits[:, :, :], bank[6][:, 0:NJ * E].rearrange("p (j e) -> p j e", j=NJ)
                                ).then_inc(dve_logits, 1)
                dve.wait_ge(dve_logits, c + 1)
                for j in range(NJ):
                    dve.max(top[:, j, :], logits[:, j, :]).then_inc(dve_top, 1)
                dve.wait_ge(dve_top, NJ * (c + 1))
                dve.tensor_tensor(gap[:, :], top[:, :, 1], top[:, :, 0], ALU.subtract).then_inc(dve_gap, 1)
                for j in range(NJ):
                    dve.max_index(topi[:, j, :], top[:, j, :], logits[:, j, :]).then_inc(dve_topi, 1)
                dve.wait_ge(dve_topi, NJ * (c + 1))
                dve.tensor_copy(topf[:, :, :], topi[:, :, :]).then_inc(dve_topf, 1)

            def feed_weights(c):
                dve.wait_ge(act_egap, c + 1)
                dve.tensor_scalar(egap1[:, :], egap[:, :], 1.0, 2.0, ALU.add, ALU.mult).then_inc(dve_e1, 1)
                dve.wait_ge(dve_e1, c + 1)
                dve.reciprocal(w_first[:, :], egap1[:, :]).then_inc(dve_w1, 1)
                dve.wait_ge(dve_w1, c + 1)
                dve.tensor_tensor(w_second[:, :], egap[:, :], w_first[:, :], ALU.mult).then_inc(dve_w2, 1)
                dve.wait_ge(dve_topf, c + 1)
                dve.wait_ge(dve_w2, c + 1)
                for j in range(NJ):
                    dve.tensor_scalar(wa[:, j, :], iota, topf[:, j, 0:1], w_first[:, j:j + 1],
                                      ALU.is_equal, ALU.mult).then_inc(dve_wab, 1)
                    dve.tensor_scalar(wb[:, j, :], iota, topf[:, j, 1:2], w_second[:, j:j + 1],
                                      ALU.is_equal, ALU.mult).then_inc(dve_wab, 1)
                dve.wait_ge(dve_wab, 2 * NJ * (c + 1))
                if c >= 1:
                    dve.wait_ge(pool_wexp, c)
                dve.tensor_tensor(wt[:, :, :], wa[:, :, :], wb[:, :, :], ALU.add).then_inc(dve_wt, 1)

            def feed_gated(c, j):
                dve.wait_ge(act_tanh, NF * c + j + 1)
                dve.scalar_tensor_tensor(out=ug[:, j % 2, :], in0=th[:, j % 2, :], scalar=1.0,
                                         in1=bank[0][:, 0:TOK], op0=ALU.add, op1=ALU.mult).then_inc(dve_up, 1)
                dve.wait_ge(dve_up, 8 * c + 2 * j + 1)
                dve.wait_ge(pe_up, 8 * c + 2 * j + 2)
                if c >= 1:
                    dve.wait_ge(pe_y, NJ * c)
                dve.tensor_tensor(sT[:, j, :], ug[:, j % 2, :], bank[1][:, 0:TOK], ALU.mult).then_inc(dve_up, 1)

            def feed_scale(c):
                for j in range(NF):
                    dve.wait_ge(pe_wbc, NF * c + j + 1)
                    dve.wait_ge(dve_up, 8 * c + 2 * j + 2)
                    dve.tensor_tensor(sT[:, j, :], sT[:, j, :], bank[4 + j % 2][:, 0:TOK], ALU.mult
                                      ).then_inc(dve_s, 1)

            def feed_out(c):
                if c >= 1:
                    dve.wait_ge(out_stored, 16 * c)
                for j in range(NJ):
                    dve.wait_ge(pe_y, NJ * c + j + 1)
                    dve.tensor_tensor(out_sb[:, j, :], bank[7 - j % 2][:, 0:D], hres[:, NJ * c + j, :], ALU.add
                                      ).then_inc(dve_y, 1)

            def shift_scores(g):
                if g >= 1:
                    dve.wait_ge(pe_pT, Q4 * g)
                    dve.wait_ge(dve_sum, Q4 * g)
                for u in range(Q4):
                    sc = bank[2 + u % 2][:, 0:NH * S].rearrange("p (n k) -> p n k", n=NH)
                    dve.wait_ge(pe_score, Q4 * g + u + 1)
                    dve.tensor_reduce(smax[:, u, :], sc, X, ALU.max).then_inc(dve_max, 1)
                    dve.wait_ge(dve_max, Q4 * g + u + 1)
                    dve.tensor_tensor(probs[:, u, :].rearrange("p (n k) -> p n k", n=NH), sc,
                                      smax[:, u, :].unsqueeze(2).to_broadcast([128, NH, S]), ALU.subtract
                                      ).then_inc(dve_sub, 1)

            def sum_probs(g):
                for u in range(Q4):
                    dve.wait_ge(act_exp, Q4 * g + u + 1)
                    dve.tensor_reduce(ssum[:, u, :], probs[:, u, :].rearrange("p (n k) -> p n k", n=NH), X, ALU.add
                                      ).then_inc(dve_sum, 1)
                dve.wait_ge(dve_sum, Q4 * (g + 1))
                dve.reciprocal(rsum[:, :, :], ssum[:, :, :]).then_inc(dve_rsum, 1)

            def scale_out(g):
                dve.wait_ge(dve_rsum, g + 1)
                if g >= 1:
                    dve.wait_ge(o_stored, 64 * g)
                for u in range(Q4):
                    dve.wait_ge(pe_o, Q4 * g + u + 1)
                    dve.tensor_tensor(o_sb[:, u, :, :].rearrange("p h n -> p n h"),
                                      bank[2 + u % 2][:, 0:D].rearrange("p (n h) -> p n h", n=NH),
                                      rsum[:, u, :].unsqueeze(2).to_broadcast([128, NH, HD]), ALU.mult
                                      ).then_inc(dve_o, 1)

            def front_begin(n):
                front_stats(n)
                front_norm(n)

            def front_end(n):
                front_stats2(n)
                front_norm2(n)

            front_begin(0)
            front_end(0)
            dve.wait_ge(act_wsum, 1)
            for i in range(G + 1):
                if i >= 1:
                    feed_residual(i - 1)
                if i + 1 < G:
                    front_stats(i + 1)
                if i >= 1:
                    feed_gate(i - 1)
                    feed_gated(i - 1, 0)
                    feed_gated(i - 1, 1)
                    feed_weights(i - 1)
                if i < G:
                    shift_scores(i)
                if i + 1 < G:
                    front_norm(i + 1)
                if i >= 1:
                    feed_gated(i - 1, 2)
                    feed_gated(i - 1, 3)
                    feed_scale(i - 1)
                if i < G:
                    sum_probs(i)
                    scale_out(i)
                if i + 1 < G:
                    front_end(i + 1)
                if i >= 1:
                    feed_out(i - 1)

        @block.tensor
        def _(pe):
            mm = pe.matmul
            pe.wait_ge(ld_small, 32)
            for t in range(S):
                last = mm(bank[t // 8][0:T, (t % 8) * C:(t % 8 + 1) * C],
                          band[:, SPAN - STRIDE * t:SPAN - STRIDE * t + T], taps[:, :], start=True, stop=True)
                if t % 8 == 7:
                    last.then_inc(pe_toep, 1)
            pe.wait_ge(act_toep, 3)
            for c in range(C):
                if c % 16 == 0:
                    pe.wait_ge(ld_x[c // 16], 16)
                last = mm(bank[3 + c // 16][0:B, (c % 16) * S:(c % 16 + 1) * S], x_sb[:, c, :], toep[:, c, :],
                          start=True, stop=True)
                if c % 16 == 15:
                    last.then_inc(pe_conv, 1)
            pe.wait_ge(ld_const, 32)
            pe.wait_ge(act_yb, 4)
            for t in range(S):
                last = pe.transpose(bank[t // 8][0:C, (t % 8) * B:(t % 8 + 1) * B], y_b[:, :, t], ident[0:B, 0:B])
                if t % 8 == 7:
                    last.then_inc(pe_yT, 1)
            pe.wait_ge(dve_ones, 2)
            pe.wait_ge(ld_front, 80)
            for k in range(2):
                last = mm(bank[7][:, 0:D], ones[:, :], wout[:, k, :], start=(k == 0), stop=(k == 1))
            last.then_inc(pe_wsum, 1)

            def front_h(n):
                pe.wait_ge(pool_ys, n + 1)
                for j in range(NJ):
                    if j == 2:
                        pe.wait_ge(act_h, NJ * n + 1)
                    elif n >= 1:
                        pe.wait_ge(act_zT, 2 * n)
                    elif j == 1:
                        pe.wait_ge(act_wsum, 1)
                    mm(bank[6 + j % 2][:, 0:D], y_stage[:, j, :, :].rearrange("c s b -> c (s b)"), wproj[:, :],
                       start=True, stop=True).then_inc(pe_h, 1)

            def front_zT(n, fed):
                pe.wait_ge(dve_z1, NJ * (n + 1))
                pe.wait_ge(act_h, NJ * (n + 1))
                for k in range(2):
                    if fed is not None:
                        pe.wait_ge(dve_y, NJ * fed + 2 + k)
                    for j in range(NJ):
                        last = pe.transpose(bank[6 + k][:, 128 * j:128 * j + 128], z1[:, j, 128 * k:128 * k + 128],
                                            ident)
                    last.then_inc(pe_zT, 1)

            def project(g):
                pe.wait_ge(act_zT, 2 * (g + 1))
                for k in range(NP):
                    if k >= 2:
                        pe.wait_ge(act_proj, NP * g + k - 1)
                    elif g == 1:
                        pe.wait_ge(act_proj, NP * g - k)
                    elif g >= 2:
                        pe.wait_ge(dve_up, 8 * (g - 1) - 1 + k)
                    for d in range(2):
                        if k < 4:
                            last = mm(bank[k % 2][:, 0:TOK], wqkv[:, d, 128 * k:128 * k + 128], zT[:, d, 0:TOK],
                                      start=(d == 0), stop=(d == 1))
                        else:
                            last = mm(bank[k % 2][:, 0:D], zT[:, d, (k - 4) * 128:(k - 3) * 128], wqkv[:, d, 2 * D:3 * D],
                                      start=(d == 0), stop=(d == 1))
                    last.then_inc(pe_proj, 1)

            def scores(g):
                pe.wait_ge(pool_kexp, 16 * (g + 1))
                pe.wait_ge(act_proj, NP * g + 4)
                for u in range(Q4):
                    if u < 2 and g >= 1:
                        pe.wait_ge(dve_o, Q4 * (g - 1) + 3 + u)
                    elif u >= 2:
                        pe.wait_ge(dve_sub, Q4 * g + u - 1)
                    mm(bank[2 + u % 2][:, 0:NH * S], identb, causal, start=True, stop=True)
                    for b4 in range(4):
                        b = 4 * u + b4
                        for k in range(2):
                            last = mm(bank[2 + u % 2][32 * b4:32 * b4 + 32, 192 * k:192 * k + 192],
                                      qT[:, k, b * S:b * S + 32], kexp[:, k, :, b * S:(b + 1) * S],
                                      start=False, stop=(k == 1), skip_group_check=True,
                                      tile_position=(0, 32 * b4))
                    last.then_inc(pe_score, 1)

            def transpose_probs(g, u):
                pe.wait_ge(act_exp, Q4 * g + u + 1)
                if u >= 2:
                    pe.wait_ge(act_pT, Q4 * g + u - 1)
                elif g >= 1:
                    pe.wait_ge(dve_s, NF * g - 1 + u)
                for n in range(4):
                    last = pe.transpose(bank[4 + u % 2][0:4 * S, 128 * n:128 * n + 128],
                                        probs[:, u, 96 * n:96 * n + 96], ident)
                last.then_inc(pe_pT, 1)

            def attend_out(g, u):
                pe.wait_ge(act_pT, Q4 * g + u + 1)
                pe.wait_ge(v_loaded, 64 * (g + 1))
                if u < 2:
                    pe.wait_ge(dve_sub, Q4 * g + 3 + u)
                else:
                    pe.wait_ge(dve_o, Q4 * g + u - 1)
                for b4 in range(4):
                    for n in range(4):
                        last = mm(bank[2 + u % 2][32 * b4:32 * b4 + 32, 64 * n:64 * n + 64],
                                  pT[:, u, n, 32 * b4:32 * b4 + 32], vdiag[:, 4 * u + b4, :, n, :],
                                  start=True, stop=True, tile_position=(0, 32 * b4))
                last.then_inc(pe_o, 1)

            def feed_z2T(c, front):
                pe.wait_ge(dve_z2, NJ * (c + 1))
                if front is not None:
                    pe.wait_ge(act_h, NJ * (front + 1))
                elif c == G - 1:
                    pe.wait_ge(dve_y, NJ * c)
                else:
                    pe.wait_ge(act_zT, 2 * G)
                for k in range(2):
                    for j in range(NJ):
                        last = pe.transpose(bank[7 - k][:, 128 * j:128 * j + 128], z2[:, j, 128 * k:128 * k + 128],
                                            ident)
                    last.then_inc(pe_z2T, 1)

            def feed_gate(c):
                pe.wait_ge(act_z2T, 2 * (c + 1))
                for k in range(2):
                    last = mm(bank[7][0:E, 0:TOK], gate[:, k, :], z2T[:, k, :], start=(k == 0), stop=(k == 1))
                last.then_inc(pe_logit, 1)

            def feed_gate_rows(c):
                pe.wait_ge(act_logit, c + 1)
                for j in range(NJ):
                    last = pe.transpose(bank[6][:, E * j:E * j + E], logitT[:, 128 * j:128 * j + 128],
                                        ident[0:E, 0:E])
                last.then_inc(pe_logits, 1)

            def feed_up(c, j, g):
                for m in range(2):
                    if j >= 1:
                        pe.wait_ge(dve_up, 8 * c + 2 * j + m - 1)
                    elif g is not None:
                        pe.wait_ge(act_proj, NP * (g + 1) - m)
                    else:
                        pe.wait_ge(dve_up, 8 * c - 1 + m)
                    for k in range(2):
                        col = m * E * R + 128 * j
                        last = mm(bank[m][:, 0:TOK], wup[:, k, col:col + 128], z2T[:, k, :],
                                  start=(k == 0), stop=(k == 1))
                    last.then_inc(pe_up, 1)

            def feed_spread(c):
                pe.wait_ge(pool_wexp, c + 1)
                for j in range(NF):
                    if j >= 2:
                        pe.wait_ge(dve_s, NF * c + j - 1)
                    else:
                        pe.wait_ge(act_pT, Q4 * (c + 1) - 1 + j)
                    for m in range(NJ):
                        last = pe.transpose(bank[4 + j % 2][:, 128 * m:128 * m + 128],
                                            wexp[:, m, 2 * j:2 * j + 2, :].rearrange("p e r -> p (e r)"), ident)
                    last.then_inc(pe_wbc, 1)

            def feed_down(c):
                pe.wait_ge(dve_s, NF * (c + 1))
                for j in range(NJ):
                    if j == 2:
                        pe.wait_ge(dve_y, NJ * c + 1)
                    for k in range(NF):
                        last = mm(bank[7 - j % 2][:, 0:D], sT[:, k, 128 * j:128 * j + 128], wdown[:, k, :],
                                  start=(k == 0), stop=(k == NF - 1))
                    last.then_inc(pe_y, 1)

            front_h(0)
            front_zT(0, None)
            pe.wait_ge(ld_qkv, 16)
            for i in range(G + 1):
                if i < G:
                    project(i)
                if i + 1 < G:
                    front_h(i + 1)
                if i >= 1:
                    if i == 1:
                        pe.wait_ge(ld_ffn, 48)
                    c = i - 1
                    feed_z2T(c, i + 1 if i + 1 < G else None)
                    feed_gate(c)
                    feed_up(c, 0, i if i < G else None)
                    feed_gate_rows(c)
                    feed_up(c, 1, i)
                if i < G:
                    scores(i)
                if i >= 1:
                    feed_up(c, 2, i)
                    feed_up(c, 3, i)
                    feed_spread(c)
                if i < G:
                    transpose_probs(i, 0)
                    transpose_probs(i, 1)
                    attend_out(i, 0)
                    transpose_probs(i, 2)
                    attend_out(i, 1)
                    transpose_probs(i, 3)
                    attend_out(i, 2)
                    attend_out(i, 3)
                if i >= 1:
                    feed_down(c)
                if i + 1 < G:
                    front_zT(i + 1, i - 1 if i >= 1 else None)


def shape_constants(np):
    size = 2 * GPAD + 1
    t = np.arange(size, dtype=np.float32) - np.float32((size - 1) / 2)
    g = np.exp(-t ** 2 / np.float32(2.0 * 2.0 ** 2)).astype(np.float32)
    g = (g / g.sum(dtype=np.float32)).astype(np.float32)
    band = np.zeros((TAPS, T + SPAN), np.float32)
    for j in range(TAPS):
        for i in range(size):
            v = SPAN - GPAD + j + i
            if 0 <= v < T + SPAN:
                band[j, v] = g[i]
    constf = np.zeros((128, 144), np.float32)
    constf[:, 0:128] = np.eye(128)
    for p in range(128):
        constf[p, 128 + p // HD] = 1.0
    constf[:, 136:144] = np.arange(8)
    from concourse import mybir as mb
    constb = np.zeros((128, 128 + NH * S), mb.dt.np(mb.dt.bfloat16))
    constb[:, 0:128] = np.eye(128)
    for p in range(128):
        q = p % 32
        if q < S:
            for n in range(NH):
                constb[p, 128 + n * S + q + 1:128 + (n + 1) * S] = -1e10
    return band, constf, constb


def kernel(**inputs):
    import numpy as np
    import concourse.bacc as bacc
    from concourse import mybir as mb
    from concourse.bass_utils import run_bass_kernel_spmd as run

    a = {k: np.asarray(v) for k, v in inputs.items()}
    band, constf, constb = shape_constants(np)
    wqkv = a["L0_attn_W_qkv"].reshape(NH, D, 3, HD)
    cols = lambda w: w.transpose(1, 0, 2).reshape(D, NH * HD)
    wv = wqkv[:, :, 2].reshape(4, 4, D, HD).transpose(2, 1, 0, 3).reshape(D, D)
    up = lambda w: w.transpose(1, 0, 2).reshape(D, E * R)
    arrays = {
        "x": a["x"].transpose(1, 2, 0),
        "band": band,
        "taps": a["L0_tok_w_temporal"].reshape(C, TAPS).T,
        "wproj": np.concatenate([a["L0_tok_w_proj"].T, a["L0_tok_b_proj"].reshape(1, D)]),
        "gamma": a["L0_tok_ln_gamma"],
        "beta": a["L0_tok_ln_beta"],
        "wqkv": np.concatenate([cols(wqkv[:, :, 1]), cols(wqkv[:, :, 0]), wv], axis=1),
        "wout": a["L0_attn_W_out"].reshape(NH * HD, D),
        "gate": a["L0_ffn_gate_w"],
        "wup": np.concatenate([up(a["L0_ffn_Wu"]), up(a["L0_ffn_Wv"])], axis=1),
        "wdown": a["L0_ffn_Wo"].reshape(E * R, D),
        "constf": constf,
        "constb": constb,
    }
    nc = bacc.Bacc("TRN2", target_bir_lowering=False, num_devices=1)
    feed, args = {}, []
    for name, v in arrays.items():
        v = np.ascontiguousarray(v)
        feed[f"in_{name}"] = v
        args.append(nc.dram_tensor(f"in_{name}", v.shape, mb.dt.from_np(v.dtype), kind="ExternalInput").ap())
    args.append(nc.dram_tensor("out_0", (B, S, D), F32, kind="ExternalOutput").ap())
    args.append(nc.dram_tensor("v_scratch", (NJ, 128, D), F32).ap())
    args.append(nc.dram_tensor("o_scratch", (Q4, 128, D), F32).ap())
    build(nc, *args)
    r = run(nc, [feed], core_ids=[0])
    return r.results[0]["out_0"]
```

```python
from contextlib import ExitStack

import concourse.bass as bass
from concourse import mybir

B, T, C = 64, 125, 64
S, D = 24, 256
NH, HD = 16, 16
E, R = 8, 64
TAPS, STRIDE, GPAD = 32, 4, 4
EPS = 1e-5
G = 4
BG = B // G
TOK = BG * S
NJ = TOK // 128
SG = S // NJ
Q4 = BG // 4
NF = E * R // 128
NP = 4 + NJ
T4 = 4
SPAN = STRIDE * T4 * (S // T4 - 1)
K_DVE, K_ACT = 5, 2
K_POOL = 8 - K_DVE - K_ACT
PAD = 8

F32 = mybir.dt.float32
F32R = mybir.dt.float32r
BF16 = mybir.dt.bfloat16
U32 = mybir.dt.uint32
ALU = mybir.AluOpType
ACT = mybir.ActivationFunctionType
X = mybir.AxisListType.X


def build(nc, x_in, band_in, taps_in, wproj_in, gamma_in, beta_in, wqkv_in, wout_in, gate_in, wup_in, wdown_in,
          constf_in, constb_in, out, v_scratch, o_scratch):
    with ExitStack() as ctx:
        def sb(name, shape, dt=F32):
            return ctx.enter_context(nc.sbuf_tensor(name, shape, dt))

        def sem(name):
            return ctx.enter_context(nc.semaphore(name))

        bank = [ctx.enter_context(nc.psum_tensor(f"bank{i}", [128, 512], F32)) for i in range(8)]

        taps_rep = sb("taps_rep", [T4 * TAPS, C])
        band = sb("band", [T4 * TAPS, T + SPAN])
        taps = sb("taps", [T4 * TAPS, T4, C])
        wqkv_hi, wqkv_lo = sb("wqkv_hi", [128, 2, 3 * D], F32R), sb("wqkv_lo", [128, 2, 3 * D], F32R)
        with nc.sbuf_tensor("x_sb", [T, C // 2, 2, B], F32) as x_sb:
            pass
        wup_hi, wup_lo = sb("wup_hi", [128, 2, 2 * E * R], F32R), sb("wup_lo", [128, 2, 2 * E * R], F32R)
        gate_hi, gate_lo = sb("gate_hi", [128, 2, E], F32R), sb("gate_lo", [128, 2, E], F32R)
        wproj = sb("wproj", [C + 1, D])
        gamma = sb("gamma", [128, D])
        beta = sb("beta", [128, D])
        wqkv = sb("wqkv", [128, 2, 3 * D])
        wout = sb("wout", [128, 2, D])
        gate = sb("gate", [128, 2, E])
        wup = sb("wup", [128, 2, 2 * E * R])
        wdown = sb("wdown", [128, NF, D])
        constf = sb("constf", [128, 144])
        constb = sb("constb", [128, 128 + NH * S], BF16)
        ident = constf[:, 0:128]
        headsel = constf[:, 128:136]
        iota = constf[:, 136:144]
        identb = constb[:, 0:128]
        causal = constb[:, 128:128 + NH * S]
        ones = sb("ones", [128, 128])
        neghalf = sb("neghalf", [128, NJ])

        toep = sb("toep", [T, C, S])
        y_b = sb("y_b", [B, C, S])
        yT = sb("yT", [C + 1, G, NJ, SG, BG])
        wsum = sb("wsum", [128, D])
        h_cent = sb("h_cent", [128, NJ, D])
        hres = sb("hres", [128, G * NJ, D])
        z1 = sb("z1", [128, NJ, D])
        zT_hi = sb("zT_hi", [128, 2, TOK], F32R)
        zT_lo = sb("zT_lo", [128, 2, TOK], F32R)
        stats = [sb(f"stats{i}", [128, NJ, 6]) for i in range(3)]
        meanvar = [sb(f"meanvar{i}", [128, NJ, 2]) for i in range(3)]
        vareps = [sb(f"vareps{i}", [128, NJ]) for i in range(3)]
        rstd = [sb(f"rstd{i}", [128, NJ]) for i in range(3)]

        kT = sb("kT", [128, 2, TOK])
        kexp = sb("kexp", [128, 2, 8, TOK])
        qT = sb("qT", [128, 2, TOK + PAD])
        v_sb = sb("v_sb", [128, NJ, D])
        vdiag = sb("vdiag", [4 * S, BG, 4, 4, HD])
        smax = sb("smax", [128, Q4, NH])
        probs = sb("probs", [128, Q4, NH * S])
        ssum = sb("ssum", [128, Q4, NH])
        rsum = sb("rsum", [128, Q4, NH])
        pT = sb("pT", [4 * S, Q4, 4, 128])
        o_sb = sb("o_sb", [128, Q4, HD, NH])

        r_sb = sb("r_sb", [128, D // NH, NJ, NH])
        rw = sb("rw", [128, NJ, D])
        z2 = sb("z2", [128, NJ, D])
        z2T_hi = sb("z2T_hi", [128, 2, TOK], F32R)
        z2T_lo = sb("z2T_lo", [128, 2, TOK], F32R)
        logitT = sb("logitT", [E, TOK])
        logits = sb("logits", [128, NJ, E])
        top = sb("top", [128, NJ, 8])
        is_a, is_b = sb("is_a", [128, NJ, E]), sb("is_b", [128, NJ, E])
        topi = sb("topi", [128, NJ, 8], U32)
        topf = sb("topf", [128, NJ, 8])
        gap = sb("gap", [128, NJ])
        egap = sb("egap", [128, NJ])
        egap1 = sb("egap1", [128, NJ])
        w_first = sb("w_first", [128, NJ])
        w_second = sb("w_second", [128, NJ])
        wa = sb("wa", [128, NJ, E])
        wb = sb("wb", [128, NJ, E])
        wt = sb("wt", [128, NJ, E])
        wexp = sb("wexp", [128, NJ, E, R])
        th = sb("th", [128, 2, TOK])
        ug = sb("ug", [128, 2, TOK])
        sT = sb("sT", [128, NF, TOK])
        out_sb = sb("out_sb", [128, NJ, D])

        ld_small = sem("ld_small")
        ld_x = [sem(f"ld_x{i}") for i in range(4)]
        ld_const = sem("ld_const")
        ld_front = sem("ld_front")
        ld_qkv = sem("ld_qkv")
        ld_ffn = sem("ld_ffn")
        v_stored = sem("v_stored")
        v_loaded = sem("v_loaded")
        o_stored = sem("o_stored")
        r_loaded = sem("r_loaded")
        out_stored = sem("out_stored")
        pe_toep, pe_conv, pe_yT, pe_wsum = sem("pe_toep"), sem("pe_conv"), sem("pe_yT"), sem("pe_wsum")
        pe_proj, pe_h, pe_zT = sem("pe_proj"), sem("pe_h"), sem("pe_zT")
        pe_z2T, pe_logit, pe_logits = sem("pe_z2T"), sem("pe_logit"), sem("pe_logits")
        pe_up, pe_score, pe_wbc = sem("pe_up"), sem("pe_score"), sem("pe_wbc")
        pe_pT, pe_o, pe_y = sem("pe_pT"), sem("pe_o"), sem("pe_y")
        act_toep, act_yb, act_yT, act_wsum = sem("act_toep"), sem("act_yb"), sem("act_yT"), sem("act_wsum")
        act_kexp, act_wexp = sem("act_kexp"), sem("act_wexp")
        act_proj, act_zT = sem("act_proj"), sem("act_zT")
        act_z2T, act_logit, act_logits, act_egap = sem("act_z2T"), sem("act_logit"), sem("act_logits"), sem("act_egap")
        act_tanh, act_exp, act_pT = sem("act_tanh"), sem("act_exp"), sem("act_pT")
        dve_ones, dve_taps = sem("dve_ones"), sem("dve_taps")
        dve_toep, dve_yb, dve_yT, dve_kexp = sem("dve_toep"), sem("dve_yb"), sem("dve_yT"), sem("dve_kexp")
        dve_cent, dve_h1 = sem("dve_cent"), sem("dve_h1")
        dve_stats = [sem(f"dve_stats{i}") for i in range(3)]
        dve_mv = [sem(f"dve_mv{i}") for i in range(3)]
        dve_z1, dve_rw, dve_h2, dve_z2 = sem("dve_z1"), sem("dve_rw"), sem("dve_h2"), sem("dve_z2")
        dve_top, dve_topi, dve_topf = sem("dve_top"), sem("dve_topi"), sem("dve_topf")
        dve_gap, dve_e1, dve_w1, dve_w2 = sem("dve_gap"), sem("dve_e1"), sem("dve_w1"), sem("dve_w2")
        dve_is = sem("dve_is")
        dve_wab, dve_wt = sem("dve_wab"), sem("dve_wt")
        dve_up, dve_s = sem("dve_up"), sem("dve_s")
        dve_max, dve_sub, dve_sum, dve_rsum, dve_o, dve_y = (
            sem("dve_max"), sem("dve_sub"), sem("dve_sum"), sem("dve_rsum"), sem("dve_o"), sem("dve_y"))
        dve_zlo, dve_z2lo = sem("dve_zlo"), sem("dve_z2lo")
        act_whi, dve_wlo, act_uphi, pool_uplo = sem("act_whi"), sem("dve_wlo"), sem("act_uphi"), sem("pool_uplo")
        pool_zero, pool_kexp = sem("pool_zero"), sem("pool_kexp")
        pool_var = [sem(f"pool_var{i}") for i in range(3)]
        pool_rstd = [sem(f"pool_rstd{i}") for i in range(3)]
        N_ZERO = 3

        def row_tile(j):
            return bank[6 + j // 2][:, (j % 2) * D:(j % 2 + 1) * D]

        def score_bank(g, u):
            return bank[(u + 2) % 4] if g == 0 else bank[2 + u % 2]

        def up_bank(j, m):
            return bank[6 * (j % 2) + m]

        def y_rows(k, m):
            rows = bank[YT_BANK[k]][0:C, m * NJ * B:(m + 1) * NJ * B]
            return (yT[0:C, :, :, 2 * k + m, :].rearrange("c g j b -> c j g b"),
                    rows.rearrange("c (j g b) -> c j g b", j=NJ, g=G))

        YT_BANK = [0, 1, 2, 5]

        block = ctx.enter_context(nc.Block())

        @block.sync
        def _(sp):
            for k in range(T4):
                sp.dma_start(taps_rep[k * TAPS:(k + 1) * TAPS, :], taps_in).then_inc(ld_small, 16)
            sp.dma_start(band[:, :], band_in).then_inc(ld_small, 16)
            for i in range(4):
                q = C // 8
                sp.dma_start(x_sb[:, i * q:(i + 1) * q, :, :], x_in[:, i * q:(i + 1) * q, :, :]
                             ).then_inc(ld_x[i], 16)
            sp.dma_start(wup[:, :, :], wup_in.rearrange("(c p) n -> p c n", p=128)).then_inc(ld_ffn, 16)
            sp.dma_start(wdown[:, :, :], wdown_in.rearrange("(c p) n -> p c n", p=128)).then_inc(ld_ffn, 16)
            sp.dma_start(gate[:, :, :], gate_in.rearrange("(c p) n -> p c n", p=128)).then_inc(ld_ffn, 16)

            def attend(g):
                sp.wait_ge(act_proj, NP * g + 2 + NJ)
                if g >= 1:
                    sp.wait_ge(v_loaded, 64 * g)
                sp.dma_start(v_scratch.rearrange("j p d -> p j d"), v_sb[:, :, :]).then_inc(v_stored, 16)
                sp.wait_ge(v_stored, 16 * (g + 1))
                sp.wait_ge(pool_zero, N_ZERO)
                if g >= 1:
                    sp.wait_ge(pe_o, Q4 * g)
                rows = v_scratch.rearrange("j p d -> (j p) d").rearrange("(b k) (n c) -> k b n c", k=S, n=4)
                for n in range(4):
                    sp.dma_start(vdiag[n * S:(n + 1) * S, :, n, :, :].rearrange("k b g h -> k b (g h)"),
                                 rows[:, :, n, :]).then_inc(v_loaded, 16)
                for u in range(Q4):
                    sp.wait_ge(dve_o, Q4 * g + u + 1)
                    if g >= 1 and u == 0:
                        sp.wait_ge(r_loaded, 16 * SG * g)
                    sp.dma_start(o_scratch[u], o_sb[:, u, :, :].rearrange("p h n -> p (h n)")).then_inc(o_stored, 16)
                sp.wait_ge(o_stored, 64 * (g + 1))
                if g >= 1:
                    sp.wait_ge(dve_rw, g)
                for k in range(SG):
                    src = bass.AP(tensor=o_scratch.tensor, offset=o_scratch.offset + k * NJ * NH,
                                  ap=[[32 * D, BG], [S * NH, D // NH], [1, NJ * NH]])
                    sp.dma_start(r_sb[k * BG:(k + 1) * BG, :, :, :].rearrange("p d j n -> p d (j n)"), src
                                 ).then_inc(r_loaded, 16)

            def store(c):
                sp.wait_ge(dve_y, NJ * (c + 1))
                dst = out[c * BG:(c + 1) * BG].rearrange("b (s j) d -> s b (j d)", j=NJ)
                sp.dma_start(dst, out_sb[:, :, :].rearrange("p j d -> p (j d)")).then_inc(out_stored, 16)

            for i in range(G + 1):
                if i < G:
                    attend(i)
                if i >= 1:
                    store(i - 1)
            sp.wait_ge(out_stored, 16 * G)

        @block.gpsimd
        def _(pool):
            pool.memset(vdiag[:, :, :, :, :], 0.0).then_inc(pool_zero, 1)
            pool.memset(qT[:, :, TOK:TOK + PAD], 0.0).then_inc(pool_zero, 1)
            pool.memset(neghalf[:, :], -0.5).then_inc(pool_zero, 1)
            pool.wait_ge(pool_zero, N_ZERO)
            pool.wait_ge(ld_const, 32)

            def rsqrt(k, n):
                pool.wait_ge(dve_mv[k], NJ * (n + 1))
                pool.tensor_scalar(vareps[k][:, :], meanvar[k][:, :, 1], EPS, None, ALU.add).then_inc(pool_var[k], 1)
                pool.wait_ge(pool_var[k], n + 1)
                pool.tensor_tensor(rstd[k][:, :], vareps[k][:, :], neghalf[:, :], ALU.pow).then_inc(pool_rstd[k], 1)

            def expand_keys(g, half):
                pool.wait_ge(act_proj, NP * g + half + 1)
                if g >= 1 and half == 0:
                    pool.wait_ge(pe_score, Q4 * g)
                for n in range(K_DVE + K_ACT, 8):
                    pool.tensor_scalar(kexp[:, half, n, :], kT[:, half, :], headsel[:, n:n + 1], None, ALU.mult
                                       ).then_inc(pool_kexp, 1)

            def split_up(k):
                pool.wait_ge(act_uphi, k + 1)
                pool.tensor_tensor(wup_lo[:, k, :], wup[:, k, :], wup_hi[:, k, :], ALU.subtract
                                   ).then_inc(pool_uplo, 1)

            rsqrt(0, 0)
            rsqrt(1, 0)
            for i in range(G + 1):
                if i < G:
                    expand_keys(i, 0)
                    expand_keys(i, 1)
                if i == 0:
                    split_up(0)
                if i >= 1:
                    rsqrt(2, i - 1)
                if i + 1 < G:
                    rsqrt(0, i + 1)
                if i == 0:
                    split_up(1)
                    pool.wait_ge(act_uphi, 3)
                    pool.tensor_tensor(gate_lo[:, :, :], gate[:, :, :], gate_hi[:, :, :], ALU.subtract
                                       ).then_inc(pool_uplo, 1)
                if i + 1 < G:
                    rsqrt(1, i + 1)

        @block.scalar
        def _(act):
            act.dma_start(constf[:, :], constf_in).then_inc(ld_const, 16)
            act.dma_start(constb[:, :], constb_in).then_inc(ld_const, 16)
            act.dma_start(wproj[:, :], wproj_in).then_inc(ld_front, 16)
            act.dma_start(gamma[:, :], gamma_in.partition_broadcast(128)).then_inc(ld_front, 16)
            act.dma_start(beta[:, :], beta_in.partition_broadcast(128)).then_inc(ld_front, 16)
            act.dma_start(wout[:, :, :], wout_in.rearrange("(c p) n -> p c n", p=128)).then_inc(ld_front, 32)
            act.dma_start(wqkv[:, :, :], wqkv_in.rearrange("(c p) n -> p c n", p=128)).then_inc(ld_qkv, 16)

            for k in (0, 2):
                act.wait_ge(pe_toep, k + 1)
                act.copy(toep[:, :, 8 * k:8 * k + 8], bank[k][0:T, :].rearrange("p (t c) -> p c t", t=8)
                         ).then_inc(act_toep, 1)
            for k in range(2):
                act.wait_ge(pe_conv, k + 1)
                act.copy(y_b[:, 16 * k:16 * k + 16, :], bank[3 + k][0:B, 0:16 * S].rearrange("p (c t) -> p c t", t=S)
                         ).then_inc(act_yb, 1)
            for k in range(0, 4, 2):
                act.wait_ge(pe_yT, k + 1)
                for m in range(2):
                    act.copy(*y_rows(k, m)).then_inc(act_yT, 1)

            def copy_wsum():
                act.wait_ge(pe_wsum, 1)
                act.copy(wsum[:, :], bank[5][:, 0:D]).then_inc(act_wsum, 1)

            ACT_KEYS = [0, 1, 2, 3, 4, 4]

            def project(g):
                for k in range(NP):
                    act.wait_ge(pe_proj, NP * g + k + 1)
                    p = bank[k % 2]
                    if k < 2:
                        if g >= 1 and k == 0:
                            act.wait_ge(pool_kexp, 2 * K_POOL * g)
                            act.wait_ge(dve_kexp, 2 * K_DVE * g)
                        ins = act.copy(kT[:, k, :], p[:, 0:TOK])
                    elif k < 2 + NJ:
                        if g >= 1:
                            act.wait_ge(v_stored, 16 * g)
                        ins = act.copy(v_sb[:, k - 2, :], p[:, 0:D])
                    else:
                        if g >= 1:
                            act.wait_ge(pe_score, Q4 * g)
                        ins = act.mul(qT[:, k - 2 - NJ, 0:TOK], p[:, 0:TOK], HD ** -0.5)
                    ins.then_inc(act_proj, 1)
                    if k >= 2:
                        if k == 2:
                            act.wait_ge(ld_const, 32)
                            act.wait_ge(act_proj, NP * g + 2)
                            if g >= 1:
                                act.wait_ge(pe_score, Q4 * g)
                        for m in range(ACT_KEYS[k - 2], ACT_KEYS[k - 1]):
                            half, n = m // K_ACT, K_DVE + m % K_ACT
                            act.activation(kexp[:, half, n, :], kT[:, half, :], ACT.Copy,
                                           scale=headsel[:, n:n + 1]).then_inc(act_kexp, 1)

            def front_zT(n):
                if n >= 1:
                    act.wait_ge(pe_proj, NP * n)
                for k in range(2):
                    act.wait_ge(pe_zT, 2 * n + k + 1)
                    act.copy(zT_hi[:, k, 0:TOK].rearrange("p (b s j) -> p j s b", b=BG, j=NJ),
                             bank[4 + k][:, 0:TOK].rearrange("p (j s b) -> p j s b", j=NJ, s=SG)
                             ).then_inc(act_zT, 1)

            def feed_z2T(c):
                for k in range(2):
                    act.wait_ge(pe_z2T, 2 * c + k + 1)
                    if c >= 1:
                        act.wait_ge(pe_up, 8 * c)
                    act.copy(z2T_hi[:, k, :], bank[4 + k][:, 0:TOK]).then_inc(act_z2T, 1)

            def feed_logit(c):
                act.wait_ge(pe_logit, c + 1)
                act.copy(logitT[:, :], bank[5][0:E, 0:TOK]).then_inc(act_logit, 1)

            def feed_logits(c):
                act.wait_ge(pe_logits, c + 1)
                if c >= 1:
                    act.wait_ge(dve_topi, NJ * c)
                act.copy(logits[:, :, :], bank[5][:, 0:NJ * E].rearrange("p (j e) -> p j e", j=NJ)
                         ).then_inc(act_logits, 1)

            def tanh(c, j):
                act.wait_ge(pe_up, 8 * c + 2 * j + 1)
                if j >= 2:
                    act.wait_ge(dve_up, 8 * c + 2 * j - 3)
                act.activation(th[:, j % 2, :], up_bank(j, 0)[:, 0:TOK], ACT.Tanh, scale=0.5).then_inc(act_tanh, 1)

            def exp_gap(c):
                act.wait_ge(dve_gap, c + 1)
                act.activation(egap[:, :], gap[:, :], ACT.Exp).then_inc(act_egap, 1)

            def expand_weights(c):
                act.wait_ge(dve_wt, c + 1)
                if c >= 1:
                    act.wait_ge(pe_wbc, NF * c)
                act.copy(wexp[:, :, :, :], wt[:, :, :].unsqueeze(3).to_broadcast([128, NJ, E, R])
                         ).then_inc(act_wexp, 1)

            def exp_scores(g, u):
                act.wait_ge(dve_sub, Q4 * g + u + 1)
                act.activation(probs[:, u, :], probs[:, u, :], ACT.Exp).then_inc(act_exp, 1)

            def evac_pT(g, u):
                act.wait_ge(pe_pT, Q4 * g + u + 1)
                if g >= 1 and u == 0:
                    act.wait_ge(pe_o, Q4 * g)
                act.copy(pT[:, u, :, :], bank[4][0:4 * S, :].rearrange("p (n q) -> p n q", n=4)
                         ).then_inc(act_pT, 1)

            copy_wsum()
            act.wait_ge(ld_qkv, 16)
            for k in range(2):
                act.copy(wqkv_hi[:, k, :], wqkv[:, k, :]).then_inc(act_whi, 1)
            act.wait_ge(ld_ffn, 48)
            for k in range(2):
                act.copy(wup_hi[:, k, :], wup[:, k, :]).then_inc(act_uphi, 1)
            act.copy(gate_hi[:, :, :], gate[:, :, :]).then_inc(act_uphi, 1)
            front_zT(0)
            for i in range(G + 1):
                attend, feed = i < G, i >= 1
                if attend:
                    project(i)
                if i == 0:
                    exp_scores(0, 0)
                    for u in range(1, Q4):
                        exp_scores(0, u)
                        evac_pT(0, u - 1)
                    evac_pT(0, Q4 - 1)
                    front_zT(1)
                    continue
                if attend:
                    exp_scores(i, 0)
                if feed:
                    feed_z2T(i - 1)
                if attend:
                    exp_scores(i, 1)
                if feed:
                    tanh(i - 1, 0)
                    feed_logit(i - 1)
                if attend:
                    evac_pT(i, 0)
                if feed:
                    tanh(i - 1, 1)
                    feed_logits(i - 1)
                if attend:
                    exp_scores(i, 2)
                if feed:
                    exp_gap(i - 1)
                if attend:
                    evac_pT(i, 1)
                    exp_scores(i, 3)
                if feed:
                    tanh(i - 1, 2)
                if attend:
                    evac_pT(i, 2)
                if feed:
                    expand_weights(i - 1)
                if attend:
                    evac_pT(i, 3)
                if feed:
                    tanh(i - 1, 3)
                if i + 1 < G:
                    front_zT(i + 1)

        @block.vector
        def _(dve):
            dve.memset(taps[:, :, :], 0.0).then_inc(dve_ones, 1)
            dve.memset(ones[:, :], 1.0).then_inc(dve_ones, 1)
            dve.memset(yT[C:C + 1, :, :, :, :], 1.0).then_inc(dve_ones, 1)

            dve.wait_ge(ld_small, 16 * (1 + T4))
            dve.wait_ge(dve_ones, 1)
            for k in range(T4):
                rows = slice(k * TAPS, (k + 1) * TAPS)
                dve.tensor_copy(taps[rows, k, :], taps_rep[rows, :]).then_inc(dve_taps, 1)
            dve.wait_ge(pe_toep, 2)
            dve.tensor_copy(toep[:, :, 8:16], bank[1][0:T, :].rearrange("p (t c) -> p c t", t=8)).then_inc(dve_toep, 1)
            for k in range(2):
                dve.wait_ge(pe_conv, k + 1)
                dve.tensor_copy(y_b[:, C // 2 + 16 * k:C // 2 + 16 * k + 16, :],
                                bank[3 + k][B:2 * B, 0:16 * S].rearrange("p (c t) -> p c t", t=S)).then_inc(dve_yb, 1)
            for k in range(1, 4, 2):
                dve.wait_ge(pe_yT, k + 1)
                for m in range(2):
                    dve.tensor_copy(*y_rows(k, m)).then_inc(dve_yT, 1)

            def layer_stats(k, n, src):
                for j in range(NJ):
                    dve.bn_stats(stats[k][:, j, :], src(j)).then_inc(dve_stats[k], 1)
                for j in range(NJ):
                    dve.wait_ge(dve_stats[k], NJ * n + j + 1)
                    dve.bn_aggr(meanvar[k][:, j, :], stats[k][:, j, :]).then_inc(dve_mv[k], 1)

            def normalise(k, n, dst, src, done):
                dve.wait_ge(pool_rstd[k], n + 1)
                for j in range(NJ):
                    dve.tensor_scalar(dst(j), src(j), meanvar[k][:, j, 0:1], rstd[k][:, j:j + 1],
                                      ALU.subtract, ALU.mult).then_inc(done, 1)

            def front_stats(n):
                dve.wait_ge(pe_h, NJ * (n + 1))
                layer_stats(0, n, row_tile)
                dve.wait_ge(dve_mv[0], NJ * (n + 1))
                for j in range(NJ):
                    dve.scalar_tensor_tensor(out=h_cent[:, j, :], in0=row_tile(j), scalar=meanvar[0][:, j, 0:1],
                                             in1=gamma[:, :], op0=ALU.subtract, op1=ALU.mult).then_inc(dve_cent, 1)

            def front_affine(n):
                dve.wait_ge(pool_rstd[0], n + 1)
                dve.wait_ge(dve_cent, NJ * (n + 1))
                for j in range(NJ):
                    dve.scalar_tensor_tensor(out=hres[:, NJ * n + j, :], in0=h_cent[:, j, :],
                                             scalar=rstd[0][:, j:j + 1], in1=beta[:, :], op0=ALU.mult, op1=ALU.add
                                             ).then_inc(dve_h1, 1)
                dve.wait_ge(dve_h1, NJ * (n + 1))
                layer_stats(1, n, lambda j: hres[:, NJ * n + j, :])

            def front_zlo(n):
                for k in range(2):
                    dve.wait_ge(act_zT, 2 * n + k + 1)
                    dve.tensor_tensor(zT_lo[:, k, 0:TOK].rearrange("p (b s j) -> p j s b", b=BG, j=NJ),
                                      bank[4 + k][:, 0:TOK].rearrange("p (j s b) -> p j s b", j=NJ, s=SG),
                                      zT_hi[:, k, 0:TOK].rearrange("p (b s j) -> p j s b", b=BG, j=NJ),
                                      ALU.subtract).then_inc(dve_zlo, 1)

            def feed_z2lo(c):
                for k in range(2):
                    dve.wait_ge(act_z2T, 2 * c + k + 1)
                    dve.tensor_tensor(z2T_lo[:, k, :], bank[4 + k][:, 0:TOK], z2T_hi[:, k, :], ALU.subtract
                                      ).then_inc(dve_z2lo, 1)

            def front_norm2(n):
                if n >= 1:
                    dve.wait_ge(pe_zT, 2 * n)
                normalise(1, n, lambda j: z1[:, j, :], lambda j: hres[:, NJ * n + j, :], dve_z1)

            def expand_keys(g):
                for half in range(2):
                    dve.wait_ge(act_proj, NP * g + half + 1)
                    if g >= 1 and half == 0:
                        dve.wait_ge(pe_score, Q4 * g)
                    for n in range(K_DVE):
                        dve.tensor_scalar(kexp[:, half, n, :], kT[:, half, :], headsel[:, n:n + 1], None, ALU.mult
                                          ).then_inc(dve_kexp, 1)

            def feed_residual(c):
                dve.wait_ge(r_loaded, 16 * SG * (c + 1))
                dve.tensor_tensor(rw[:, :, :].rearrange("p j (n d) -> p j n d", n=NH),
                                  r_sb[:, :, :, :].rearrange("p d j n -> p j n d"),
                                  wsum[:, :].rearrange("p (n d) -> p n d", n=NH).unsqueeze(1)
                                  .to_broadcast([128, NJ, NH, D // NH]), ALU.mult).then_inc(dve_rw, 1)
                dve.wait_ge(dve_rw, c + 1)
                h = hres[:, NJ * c:NJ * c + NJ, :]
                dve.tensor_tensor(h, h, rw[:, :, :], ALU.add).then_inc(dve_h2, 1)
                dve.wait_ge(dve_h2, c + 1)
                layer_stats(2, c, lambda j: hres[:, NJ * c + j, :])

            def feed_norm(c):
                if c >= 1:
                    dve.wait_ge(pe_z2T, 2 * c)
                normalise(2, c, lambda j: z2[:, j, :], lambda j: hres[:, NJ * c + j, :], dve_z2)

            def feed_gate(c):
                dve.wait_ge(act_logits, c + 1)
                for j in range(NJ):
                    dve.max(top[:, j, :], logits[:, j, :]).then_inc(dve_top, 1)
                dve.wait_ge(dve_top, NJ * (c + 1))
                dve.tensor_tensor(gap[:, :], top[:, :, 1], top[:, :, 0], ALU.subtract).then_inc(dve_gap, 1)
                for j in range(NJ):
                    dve.max_index(topi[:, j, :], top[:, j, :], logits[:, j, :]).then_inc(dve_topi, 1)
                dve.wait_ge(dve_topi, NJ * (c + 1))
                dve.tensor_copy(topf[:, :, :], topi[:, :, :]).then_inc(dve_topf, 1)

            def feed_weights(c):
                dve.wait_ge(act_egap, c + 1)
                dve.tensor_scalar(egap1[:, :], egap[:, :], 1.0, 2.0, ALU.add, ALU.mult).then_inc(dve_e1, 1)
                dve.wait_ge(dve_e1, c + 1)
                dve.reciprocal(w_first[:, :], egap1[:, :]).then_inc(dve_w1, 1)
                dve.wait_ge(dve_w1, c + 1)
                dve.tensor_tensor(w_second[:, :], egap[:, :], w_first[:, :], ALU.mult).then_inc(dve_w2, 1)
                dve.wait_ge(dve_topf, c + 1)
                dve.wait_ge(dve_w2, c + 1)
                every = lambda ap: ap.unsqueeze(2).to_broadcast([128, NJ, E])
                number = iota.unsqueeze(1).to_broadcast([128, NJ, E])
                dve.tensor_tensor(is_a[:, :, :], number, every(topf[:, :, 0]), ALU.is_equal).then_inc(dve_is, 1)
                dve.tensor_tensor(is_b[:, :, :], number, every(topf[:, :, 1]), ALU.is_equal).then_inc(dve_is, 1)
                dve.wait_ge(dve_is, 2 * c + 1)
                dve.tensor_tensor(wa[:, :, :], is_a[:, :, :], every(w_first[:, :]), ALU.mult).then_inc(dve_wab, 1)
                dve.wait_ge(dve_is, 2 * c + 2)
                dve.tensor_tensor(wb[:, :, :], is_b[:, :, :], every(w_second[:, :]), ALU.mult).then_inc(dve_wab, 1)
                dve.wait_ge(dve_wab, 2 * (c + 1))
                if c >= 1:
                    dve.wait_ge(act_wexp, c)
                dve.tensor_tensor(wt[:, :, :], wa[:, :, :], wb[:, :, :], ALU.add).then_inc(dve_wt, 1)

            def feed_gated(c, j):
                dve.wait_ge(act_tanh, NF * c + j + 1)
                dve.scalar_tensor_tensor(out=ug[:, j % 2, :], in0=th[:, j % 2, :], scalar=1.0,
                                         in1=up_bank(j, 0)[:, 0:TOK], op0=ALU.add, op1=ALU.mult).then_inc(dve_up, 1)
                dve.wait_ge(dve_up, 8 * c + 2 * j + 1)
                dve.wait_ge(pe_up, 8 * c + 2 * j + 2)
                if c >= 1:
                    dve.wait_ge(pe_y, NJ * c)
                dve.tensor_tensor(sT[:, j, :], ug[:, j % 2, :], up_bank(j, 1)[:, 0:TOK], ALU.mult).then_inc(dve_up, 1)

            def feed_scale(c, j):
                dve.wait_ge(pe_wbc, NF * c + j + 1)
                dve.wait_ge(dve_up, 8 * c + 2 * j + 2)
                dve.tensor_tensor(sT[:, j, :], sT[:, j, :], bank[2 + j % 2][:, 0:TOK], ALU.mult).then_inc(dve_s, 1)

            def feed_out(c):
                if c >= 1:
                    dve.wait_ge(out_stored, 16 * c)
                for j in (2, 0, 1):
                    dve.wait_ge(pe_y, NJ * c + (1 if j == 2 else NJ))
                    dve.tensor_tensor(out_sb[:, j, :], row_tile(j), hres[:, NJ * c + j, :], ALU.add
                                      ).then_inc(dve_y, 1)

            def shift_scores(g, u):
                if g >= 1 and u == 0:
                    dve.wait_ge(pe_pT, Q4 * g)
                sc = score_bank(g, u)[:, 0:NH * S].rearrange("p (n k) -> p n k", n=NH)
                dve.wait_ge(pe_score, Q4 * g + u + 1)
                dve.tensor_reduce(smax[:, u, :], sc, X, ALU.max).then_inc(dve_max, 1)
                dve.wait_ge(dve_max, Q4 * g + u + 1)
                dve.tensor_tensor(probs[:, u, :].rearrange("p (n k) -> p n k", n=NH), sc,
                                  smax[:, u, :].unsqueeze(2).to_broadcast([128, NH, S]), ALU.subtract
                                  ).then_inc(dve_sub, 1)

            def sum_probs(g, u):
                dve.wait_ge(act_exp, Q4 * g + u + 1)
                dve.tensor_reduce(ssum[:, u, :], probs[:, u, :].rearrange("p (n k) -> p n k", n=NH), X, ALU.add
                                  ).then_inc(dve_sum, 1)
                dve.wait_ge(dve_sum, Q4 * g + u + 1)
                dve.reciprocal(rsum[:, u, :], ssum[:, u, :]).then_inc(dve_rsum, 1)

            def scale_out(g, u):
                dve.wait_ge(dve_rsum, Q4 * g + u + 1)
                if g >= 1 and u == 0:
                    dve.wait_ge(o_stored, 64 * g)
                dve.wait_ge(pe_o, Q4 * g + u + 1)
                dve.tensor_tensor(o_sb[:, u, :, :].rearrange("p h n -> p n h"),
                                  bank[5][:, 0:D].rearrange("p (n h) -> p n h", n=NH),
                                  rsum[:, u, :].unsqueeze(2).to_broadcast([128, NH, HD]), ALU.mult
                                  ).then_inc(dve_o, 1)

            dve.wait_ge(ld_front, 80)
            front_stats(0)
            front_affine(0)
            front_norm2(0)
            for k in range(2):
                dve.wait_ge(act_whi, k + 1)
                dve.tensor_tensor(wqkv_lo[:, k, :], wqkv[:, k, :], wqkv_hi[:, k, :], ALU.subtract).then_inc(dve_wlo, 1)
            front_zlo(0)
            dve.wait_ge(ld_const, 32)
            for i in range(G + 1):
                attend, front, feed = i < G, i + 1 < G, i >= 1
                if i == 1:
                    dve.wait_ge(act_wsum, 1)
                if attend:
                    expand_keys(i)
                if i == 0:
                    for u in range(Q4):
                        shift_scores(0, u)
                    front_stats(1)
                    sum_probs(0, 0)
                    scale_out(0, 0)
                    sum_probs(0, 1)
                    front_affine(1)
                    scale_out(0, 1)
                    for u in range(2, Q4):
                        sum_probs(0, u)
                        scale_out(0, u)
                    front_norm2(1)
                    front_zlo(1)
                    continue
                if feed:
                    feed_residual(i - 1)
                    feed_norm(i - 1)
                if attend:
                    shift_scores(i, 0)
                    shift_scores(i, 1)
                if feed:
                    feed_z2lo(i - 1)
                if front:
                    front_stats(i + 1)
                if feed:
                    feed_gated(i - 1, 0)
                if attend:
                    sum_probs(i, 0)
                if front:
                    front_affine(i + 1)
                if attend:
                    shift_scores(i, 2)
                if feed:
                    feed_gate(i - 1)
                    feed_gated(i - 1, 1)
                if attend:
                    scale_out(i, 0)
                    sum_probs(i, 1)
                    shift_scores(i, 3)
                if feed:
                    feed_weights(i - 1)
                if attend:
                    scale_out(i, 1)
                if feed:
                    feed_gated(i - 1, 2)
                if attend:
                    sum_probs(i, 2)
                    scale_out(i, 2)
                    sum_probs(i, 3)
                    scale_out(i, 3)
                if feed:
                    feed_gated(i - 1, 3)
                    feed_scale(i - 1, 0)
                    feed_scale(i - 1, 1)
                if front:
                    front_norm2(i + 1)
                if feed:
                    feed_scale(i - 1, 2)
                    feed_scale(i - 1, 3)
                if front:
                    front_zlo(i + 1)
                if feed:
                    feed_out(i - 1)

        @block.tensor
        def _(pe):
            mm = pe.matmul
            pe.wait_ge(ld_small, 16 * (1 + T4))
            pe.wait_ge(dve_taps, T4)
            for k in range(S // T4):
                shift = SPAN - STRIDE * T4 * k
                last = mm(bank[k // 2][0:T, (k % 2) * T4 * C:(k % 2 + 1) * T4 * C], band[:, shift:shift + T],
                          taps[:, :, :].rearrange("j t c -> j (t c)"), start=True, stop=True)
                if k % 2:
                    last.then_inc(pe_toep, 1)
            pe.wait_ge(act_toep, 2)
            pe.wait_ge(dve_toep, 1)
            for c in range(C // 2):
                if c % 8 == 0:
                    pe.wait_ge(ld_x[c // 8], 16)
                for h in range(2):
                    for q in range(2):
                        row = 64 * h + 32 * q
                        last = mm(bank[3 + c // 16][row:row + 32, (c % 16) * S:(c % 16 + 1) * S],
                                  x_sb[:, c, h, 32 * q:32 * q + 32], toep[:, h * C // 2 + c, :],
                                  start=True, stop=True, tile_position=(0, row))
                if c % 16 == 15:
                    last.then_inc(pe_conv, 1)
            pe.wait_ge(ld_const, 32)
            pe.wait_ge(act_yb, 2)
            pe.wait_ge(dve_yb, 2)
            for t in range(S):
                last = pe.transpose(bank[YT_BANK[t // 6]][0:C, (t % 6) * B:(t % 6 + 1) * B], y_b[:, :, t],
                                    ident[0:B, 0:B])
                if t % 6 == 5:
                    last.then_inc(pe_yT, 1)

            def sum_wout():
                for k in range(2):
                    last = mm(bank[5][:, 0:D], ones[:, :], wout[:, k, :], start=(k == 0), stop=(k == 1))
                last.then_inc(pe_wsum, 1)

            def front_h(n):
                if n == 0:
                    pe.wait_ge(act_yT, 4)
                    pe.wait_ge(dve_yT, 4)
                    pe.wait_ge(dve_ones, 3)
                if n >= 3:
                    pe.wait_ge(dve_y, NJ * (n - 2))
                elif n >= 1:
                    pe.wait_ge(dve_cent, NJ * n)
                for j in range(NJ):
                    mm(row_tile(j), yT[:, n, j, :, :].rearrange("c s b -> c (s b)"), wproj[:, :],
                       start=True, stop=True).then_inc(pe_h, 1)

            def front_zT(n):
                pe.wait_ge(dve_z1, NJ * (n + 1))
                if n >= 1:
                    pe.wait_ge(act_pT, Q4 * n)
                    pe.wait_ge(dve_o, Q4 * n)
                else:
                    pe.wait_ge(act_wsum, 1)
                for k in range(2):
                    for j in range(NJ):
                        last = pe.transpose(bank[4 + k][:, 128 * j:128 * j + 128], z1[:, j, 128 * k:128 * k + 128],
                                            ident)
                    last.then_inc(pe_zT, 1)

            def project(g):
                pe.wait_ge(act_zT, 2 * (g + 1))
                pe.wait_ge(dve_wlo, 2)
                for k in range(NP):
                    if k >= 2:
                        pe.wait_ge(act_proj, NP * g + k - 1)
                    elif g == 1:
                        pe.wait_ge(dve_sub, 3 + k)
                    elif g >= 2:
                        pe.wait_ge(dve_up, 8 * (g - 1) - 3 + k)
                    for p, (w, z) in enumerate(((wqkv_hi, zT_hi), (wqkv_lo, zT_hi), (wqkv_hi, zT_lo))):
                        if p == 2:
                            pe.wait_ge(dve_zlo, 2 * (g + 1))
                        for d in range(2):
                            first, final = p == 0 and d == 0, p == 2 and d == 1
                            if 2 <= k < 2 + NJ:
                                last = mm(bank[k % 2][:, 0:D], z[:, d, (k - 2) * 128:(k - 1) * 128],
                                          w[:, d, 2 * D:3 * D], start=first, stop=final)
                            else:
                                col = 128 * k if k < 2 else D + 128 * (k - 2 - NJ)
                                last = mm(bank[k % 2][:, 0:TOK], w[:, d, col:col + 128], z[:, d, :],
                                          start=first, stop=final)
                    last.then_inc(pe_proj, 1)

            def scores(g, u):
                if u == 0:
                    pe.wait_ge(dve_kexp, 2 * K_DVE * (g + 1))
                    pe.wait_ge(act_kexp, 2 * K_ACT * (g + 1))
                    pe.wait_ge(pool_kexp, 2 * K_POOL * (g + 1))
                    pe.wait_ge(pool_zero, N_ZERO)
                    pe.wait_ge(act_proj, NP * g + NP)
                if g >= 1 and u >= 2:
                    pe.wait_ge(dve_sub, Q4 * g + u - 1)
                elif g >= 2:
                    pe.wait_ge(dve_s, NF * (g - 1) - 1 + u)
                elif g == 1:
                    pe.wait_ge(dve_sub, u + 1)
                mm(score_bank(g, u)[:, 0:NH * S], identb, causal, start=True, stop=True)
                for k in range(2):
                    for b4 in range(4):
                        b = 4 * u + b4
                        last = mm(score_bank(g, u)[32 * b4:32 * b4 + 32, 192 * k:192 * k + 192],
                                  qT[:, k, b * S:b * S + 32], kexp[:, k, :, b * S:(b + 1) * S],
                                  start=False, stop=True, skip_group_check=True, tile_position=(0, 32 * b4))
                last.then_inc(pe_score, 1)

            def transpose_probs(g, u):
                pe.wait_ge(act_exp, Q4 * g + u + 1)
                if u >= 1:
                    pe.wait_ge(act_pT, Q4 * g + u)
                elif g >= 1:
                    pe.wait_ge(dve_z2lo, 2 * g)
                else:
                    pe.wait_ge(dve_zlo, 2)
                for n in range(4):
                    last = pe.transpose(bank[4][0:4 * S, 128 * n:128 * n + 128],
                                        probs[:, u, 96 * n:96 * n + 96], ident)
                last.then_inc(pe_pT, 1)

            def attend_out(g, u):
                pe.wait_ge(act_pT, Q4 * g + u + 1)
                pe.wait_ge(v_loaded, 64 * (g + 1))
                if u >= 1:
                    pe.wait_ge(dve_o, Q4 * g + u)
                elif g >= 1:
                    pe.wait_ge(act_logits, g)
                else:
                    pe.wait_ge(dve_zlo, 2)
                for n in range(4):
                    for b4 in range(4):
                        last = mm(bank[5][32 * b4:32 * b4 + 32, 64 * n:64 * n + 64],
                                  pT[:, u, n, 32 * b4:32 * b4 + 32], vdiag[:, 4 * u + b4, :, n, :],
                                  start=True, stop=True, tile_position=(0, 32 * b4))
                last.then_inc(pe_o, 1)

            def feed_z2T(c):
                pe.wait_ge(dve_z2, NJ * (c + 1))
                if c + 1 < G:
                    pe.wait_ge(dve_zlo, 2 * (c + 2))
                else:
                    pe.wait_ge(act_pT, Q4 * G)
                    pe.wait_ge(dve_o, Q4 * G)
                for k in range(2):
                    for j in range(NJ):
                        last = pe.transpose(bank[4 + k][:, 128 * j:128 * j + 128], z2[:, j, 128 * k:128 * k + 128],
                                            ident)
                    last.then_inc(pe_z2T, 1)

            def feed_logit(c):
                pe.wait_ge(pool_uplo, 3)
                pe.wait_ge(dve_z2lo, 2 * (c + 1))
                for p, (w, z) in enumerate(((gate_hi, z2T_hi), (gate_lo, z2T_hi), (gate_hi, z2T_lo))):
                    for k in range(2):
                        last = mm(bank[5][0:E, 0:TOK], w[:, k, :], z[:, k, :],
                                  start=(p == 0 and k == 0), stop=(p == 2 and k == 1))
                last.then_inc(pe_logit, 1)

            def feed_logits(c):
                pe.wait_ge(act_logit, c + 1)
                for j in range(NJ):
                    last = pe.transpose(bank[5][:, E * j:E * j + E], logitT[:, 128 * j:128 * j + 128],
                                        ident[0:E, 0:E])
                last.then_inc(pe_logits, 1)

            def feed_up(c, j, parts=(0, 1)):
                for m in parts:
                    if j >= 2:
                        pe.wait_ge(dve_up, 8 * c + 2 * (j - 2) + m + 1)
                    elif j == 1 and c + 2 < G:
                        pe.wait_ge(dve_cent, NJ * (c + 3))
                    elif j == 1:
                        pe.wait_ge(dve_y, NJ * c)
                    elif c + 1 < G:
                        pe.wait_ge(act_proj, NP * (c + 2) - m)
                    else:
                        pe.wait_ge(dve_up, 8 * c - 3 + m)
                    col = m * E * R + 128 * j
                    for p, (w, z) in enumerate(((wup_hi, z2T_hi), (wup_lo, z2T_hi), (wup_hi, z2T_lo))):
                        if j == 0 and p < 2:
                            pe.wait_ge((act_z2T, pool_uplo)[p], (2 * (c + 1), 3)[p])
                        elif j == 0:
                            pe.wait_ge(dve_z2lo, 2 * (c + 1))
                        for k in range(2):
                            last = mm(up_bank(j, m)[:, 0:TOK], w[:, k, col:col + 128], z[:, k, :],
                                      start=(p == 0 and k == 0), stop=(p == 2 and k == 1))
                    last.then_inc(pe_up, 1)

            def feed_spread(c, j):
                pe.wait_ge(act_wexp, c + 1)
                if j >= 2:
                    pe.wait_ge(dve_s, NF * c + j - 1)
                elif c + 1 < G:
                    pe.wait_ge(dve_sub, Q4 * (c + 1) + 3 + j)
                else:
                    pe.wait_ge(dve_s, NF * c - 1 + j)
                for m in range(NJ):
                    last = pe.transpose(bank[2 + j % 2][:, 128 * m:128 * m + 128],
                                        wexp[:, m, 2 * j:2 * j + 2, :].rearrange("p e r -> p (e r)"), ident)
                last.then_inc(pe_wbc, 1)

            def feed_down(c):
                pe.wait_ge(dve_s, NF * (c + 1))
                for j in (2, 0, 1):
                    for k in range(NF):
                        last = mm(row_tile(j), sT[:, k, 128 * j:128 * j + 128], wdown[:, k, :],
                                  start=(k == 0), stop=(k == NF - 1))
                    last.then_inc(pe_y, 1)

            pe.wait_ge(ld_front, 80)
            front_h(0)
            sum_wout()
            front_zT(0)
            pe.wait_ge(ld_qkv, 16)
            for i in range(G + 1):
                attend, front, feed = i < G, i + 1 < G, i >= 1
                if attend:
                    project(i)
                if i == 0:
                    front_h(1)
                    for u in range(Q4):
                        scores(0, u)
                    transpose_probs(0, 0)
                    for u in range(1, Q4):
                        transpose_probs(0, u)
                        attend_out(0, u - 1)
                    attend_out(0, Q4 - 1)
                    front_zT(1)
                    continue
                if attend:
                    scores(i, 0)
                    scores(i, 1)
                if i == 1:
                    pe.wait_ge(ld_ffn, 48)
                if feed:
                    feed_z2T(i - 1)
                if front:
                    front_h(i + 1)
                if feed:
                    feed_up(i - 1, 0, [0])
                    feed_logit(i - 1)
                    feed_up(i - 1, 0, [1])
                if attend:
                    transpose_probs(i, 0)
                if feed:
                    feed_up(i - 1, 1, [0])
                if attend:
                    scores(i, 2)
                if feed:
                    feed_logits(i - 1)
                    feed_up(i - 1, 1, [1])
                if attend:
                    attend_out(i, 0)
                    transpose_probs(i, 1)
                    scores(i, 3)
                if feed:
                    feed_up(i - 1, 2, [0])
                if attend:
                    attend_out(i, 1)
                    transpose_probs(i, 2)
                if feed:
                    feed_up(i - 1, 2, [1])
                if attend:
                    attend_out(i, 2)
                    transpose_probs(i, 3)
                if feed:
                    feed_up(i - 1, 3, [0])
                if attend:
                    attend_out(i, 3)
                if feed:
                    feed_up(i - 1, 3, [1])
                    for j in range(NF):
                        feed_spread(i - 1, j)
                if front:
                    front_zT(i + 1)
                if feed:
                    feed_down(i - 1)


def shape_constants(np):
    size = 2 * GPAD + 1
    t = np.arange(size, dtype=np.float32) - np.float32((size - 1) / 2)
    g = np.exp(-t ** 2 / np.float32(2.0 * 2.0 ** 2)).astype(np.float32)
    g = (g / g.sum(dtype=np.float32)).astype(np.float32)
    band = np.zeros((T4 * TAPS, T + SPAN), np.float32)
    for k in range(T4):
        for j in range(TAPS):
            for i in range(size):
                v = SPAN - GPAD + STRIDE * k + j + i
                if 0 <= v < T + SPAN:
                    band[k * TAPS + j, v] = g[i]
    constf = np.zeros((128, 144), np.float32)
    constf[:, 0:128] = np.eye(128)
    for p in range(128):
        constf[p, 128 + p // HD] = 1.0
    constf[:, 136:144] = np.arange(8)
    from concourse import mybir as mb
    constb = np.zeros((128, 128 + NH * S), mb.dt.np(mb.dt.bfloat16))
    constb[:, 0:128] = np.eye(128)
    for p in range(128):
        q = p % 32
        if q < S:
            for n in range(NH):
                constb[p, 128 + n * S + q + 1:128 + (n + 1) * S] = -1e10
    return band, constf, constb


def kernel(**inputs):
    import numpy as np
    import concourse.bacc as bacc
    from concourse import mybir as mb
    from concourse.bass_utils import run_bass_kernel_spmd as run

    a = {k: np.asarray(v) for k, v in inputs.items()}
    band, constf, constb = shape_constants(np)
    wqkv = a["L0_attn_W_qkv"].reshape(NH, D, 3, HD)
    cols = lambda w: w.transpose(1, 0, 2).reshape(D, NH * HD)
    wv = wqkv[:, :, 2].reshape(4, 4, D, HD).transpose(2, 1, 0, 3).reshape(D, D)
    up = lambda w: w.transpose(1, 0, 2).reshape(D, E * R)
    arrays = {
        "x": a["x"].transpose(1, 2, 0).reshape(T, 2, C // 2, B).transpose(0, 2, 1, 3),
        "band": band,
        "taps": a["L0_tok_w_temporal"].reshape(C, TAPS).T,
        "wproj": np.concatenate([a["L0_tok_w_proj"].T, a["L0_tok_b_proj"].reshape(1, D)]),
        "gamma": a["L0_tok_ln_gamma"],
        "beta": a["L0_tok_ln_beta"],
        "wqkv": np.concatenate([cols(wqkv[:, :, 1]), cols(wqkv[:, :, 0]), wv], axis=1),
        "wout": a["L0_attn_W_out"].reshape(NH * HD, D),
        "gate": a["L0_ffn_gate_w"],
        "wup": np.concatenate([up(a["L0_ffn_Wu"]), up(a["L0_ffn_Wv"])], axis=1),
        "wdown": a["L0_ffn_Wo"].reshape(E * R, D),
        "constf": constf,
        "constb": constb,
    }
    nc = bacc.Bacc("TRN2", target_bir_lowering=False, num_devices=1)
    feed, args = {}, []
    for name, v in arrays.items():
        v = np.ascontiguousarray(v)
        feed[f"in_{name}"] = v
        args.append(nc.dram_tensor(f"in_{name}", v.shape, mb.dt.from_np(v.dtype), kind="ExternalInput").ap())
    args.append(nc.dram_tensor("out_0", (B, S, D), F32, kind="ExternalOutput").ap())
    args.append(nc.dram_tensor("v_scratch", (NJ, 128, D), F32).ap())
    args.append(nc.dram_tensor("o_scratch", (Q4, 128, D), F32).ap())
    build(nc, *args)
    r = run(nc, [feed], core_ids=[0])
    return r.results[0]["out_0"]
```

```python
from contextlib import ExitStack

import concourse.bass as bass
from concourse import mybir

B, T, C = 64, 125, 64
S, D = 24, 256
NH, HD = 16, 16
E, R = 8, 64
TAPS, STRIDE, GPAD = 32, 4, 4
EPS = 1e-5
G = 4
BG = B // G
TOK = BG * S
NJ = TOK // 128
SG = S // NJ
Q4 = BG // 4
NF = E * R // 128
NP = 4 + NJ
T4 = 4
SPAN = STRIDE * T4 * (S // T4 - 1)
K_DVE, K_ACT = 5, 2
K_POOL = 8 - K_DVE - K_ACT
OW = 5 * HD
PAD = 8

F32 = mybir.dt.float32
F32R = mybir.dt.float32r
BF16 = mybir.dt.bfloat16
U32 = mybir.dt.uint32
ALU = mybir.AluOpType
ACT = mybir.ActivationFunctionType
X = mybir.AxisListType.X


def build(nc, x_in, band_in, taps_in, wproj_in, gamma_in, beta_in, wqkv_in, wout_in, gate_in, wup_in, wdown_in,
          constf_in, constb_in, out, v_scratch, o_scratch):
    with ExitStack() as ctx:
        def sb(name, shape, dt=F32):
            return ctx.enter_context(nc.sbuf_tensor(name, shape, dt))

        def sem(name):
            return ctx.enter_context(nc.semaphore(name))

        bank = [ctx.enter_context(nc.psum_tensor(f"bank{i}", [128, 512], F32)) for i in range(8)]

        taps_rep = sb("taps_rep", [T4 * TAPS, C])
        band = sb("band", [T4 * TAPS, T + SPAN])
        taps = sb("taps", [T4 * TAPS, T4, C])
        wqkv_hi, wqkv_lo = sb("wqkv_hi", [128, 2, 3 * D], F32R), sb("wqkv_lo", [128, 2, 3 * D], F32R)
        with (nc.sbuf_tensor("x_sb", [T, 2, C // 2, 2, 32], F32) as x_sb,
              nc.sbuf_tensor("toep", [T, C, S], F32) as toep):
            pass
        wup_hi, wup_lo = sb("wup_hi", [128, 2, 2 * E * R], F32R), sb("wup_lo", [128, 2, 2 * E * R], F32R)
        rw = sb("rw", [128, NJ, D])
        z2 = sb("z2", [128, NJ, D])
        gate_hi, gate_lo = sb("gate_hi", [128, 2, E], F32R), sb("gate_lo", [128, 2, E], F32R)
        wproj = sb("wproj", [C + 1, D])
        gamma = sb("gamma", [128, D])
        beta = sb("beta", [128, D])
        wqkv = sb("wqkv", [128, 2, 3 * D])
        wout = sb("wout", [128, 2, D])
        gate = sb("gate", [128, 2, E])
        wup = sb("wup", [128, 2, 2 * E * R])
        wdown = sb("wdown", [128, NF, D])
        constf = sb("constf", [128, 148])
        constb = sb("constb", [128, 128 + NH * S], BF16)
        ident = constf[:, 0:128]
        headsel = constf[:, 128:136]
        iota = constf[:, 136:144]
        keysel = constf[0:4 * S, 144:148]
        identb = constb[:, 0:128]
        causal = constb[:, 128:128 + NH * S]
        ones = sb("ones", [128, 128])
        neghalf = sb("neghalf", [128, NJ])

        y_b = sb("y_b", [B, C, S])
        yT = sb("yT", [C + 1, G, NJ, SG, BG])
        wsum = sb("wsum", [128, D])
        h_cent = sb("h_cent", [128, NJ, D])
        hres = sb("hres", [128, G * NJ, D])
        z1 = sb("z1", [128, NJ, D])
        zT_hi = sb("zT_hi", [128, 2, TOK], F32R)
        zT_lo = sb("zT_lo", [128, 2, TOK], F32R)
        stats = [sb(f"stats{i}", [128, NJ, 6]) for i in range(3)]
        meanvar = [sb(f"meanvar{i}", [128, NJ, 2]) for i in range(3)]
        vareps = [sb(f"vareps{i}", [128, NJ]) for i in range(3)]
        shift1 = sb("shift1", [128, NJ])
        rstd = [sb(f"rstd{i}", [128, NJ]) for i in range(3)]

        kT = sb("kT", [128, 2, TOK])
        kexp = sb("kexp", [128, 2, 8, TOK])
        qT = sb("qT", [128, 2, TOK + PAD])
        v_sb = sb("v_sb", [128, NJ, D])
        vdiag = sb("vdiag", [4 * S, BG, 5, 4, HD])
        smax = sb("smax", [128, Q4, NH])
        probs = sb("probs", [128, Q4, NH * S])
        rsum = sb("rsum", [128, Q4, 4, 4])
        pT = sb("pT", [4 * S, Q4, 4, 128])
        o_sb = sb("o_sb", [128, Q4, HD, NH])

        r_sb = sb("r_sb", [128, D // NH, NJ, NH])
        z2T_hi = sb("z2T_hi", [128, 2, TOK], F32R)
        z2T_lo = sb("z2T_lo", [128, 2, TOK], F32R)
        logitT = sb("logitT", [E, TOK])
        logits = sb("logits", [128, NJ, E])
        top = sb("top", [128, NJ, 8])
        is_a, is_b = sb("is_a", [128, NJ, E]), sb("is_b", [128, NJ, E])
        topi = sb("topi", [128, NJ, 8], U32)
        topf = sb("topf", [128, NJ, 8])
        gap = sb("gap", [128, NJ])
        egap = sb("egap", [128, NJ])
        egap1 = sb("egap1", [128, NJ])
        w_first = sb("w_first", [128, NJ])
        w_second = sb("w_second", [128, NJ])
        wa = sb("wa", [128, NJ, E])
        wb = sb("wb", [128, NJ, E])
        wt = sb("wt", [128, NJ, E])
        wexp = sb("wexp", [128, NJ, E, R])
        th = sb("th", [128, 2, TOK])
        ug = sb("ug", [128, 2, TOK])
        sT = sb("sT", [128, NF, TOK])
        out_sb = sb("out_sb", [128, NJ, D])

        ld_small = sem("ld_small")
        ld_x = [sem(f"ld_x{i}") for i in range(4)]
        ld_const = sem("ld_const")
        ld_front = sem("ld_front")
        ld_wout = sem("ld_wout")
        ld_qkv = sem("ld_qkv")
        ld_ffn = sem("ld_ffn")
        v_stored = sem("v_stored")
        v_loaded = sem("v_loaded")
        o_stored = sem("o_stored")
        r_loaded = sem("r_loaded")
        out_stored = sem("out_stored")
        pe_toep, pe_conv, pe_yT, pe_wsum = sem("pe_toep"), sem("pe_conv"), sem("pe_yT"), sem("pe_wsum")
        pe_proj, pe_h, pe_zT = sem("pe_proj"), sem("pe_h"), sem("pe_zT")
        pe_z2T, pe_logit, pe_logits = sem("pe_z2T"), sem("pe_logit"), sem("pe_logits")
        pe_up, pe_score, pe_wbc = sem("pe_up"), sem("pe_score"), sem("pe_wbc")
        pe_pT, pe_o, pe_y = sem("pe_pT"), sem("pe_o"), sem("pe_y")
        act_table = sem("act_table")
        act_toep, act_yb, act_yT, act_wsum = sem("act_toep"), sem("act_yb"), sem("act_yT"), sem("act_wsum")
        act_kexp, act_wexp = sem("act_kexp"), sem("act_wexp")
        act_proj, act_z1, act_zT = sem("act_proj"), sem("act_z1"), sem("act_zT")
        act_z2T, act_logit, act_logits, act_egap = sem("act_z2T"), sem("act_logit"), sem("act_logits"), sem("act_egap")
        act_tanh, act_exp, act_pT = sem("act_tanh"), sem("act_exp"), sem("act_pT")
        dve_ones, dve_taps = sem("dve_ones"), sem("dve_taps")
        dve_toep, dve_yb, dve_yT, dve_kexp = sem("dve_toep"), sem("dve_yb"), sem("dve_yT"), sem("dve_kexp")
        dve_cent, dve_h1 = sem("dve_cent"), sem("dve_h1")
        dve_stats = [sem(f"dve_stats{i}") for i in range(3)]
        dve_mv = [sem(f"dve_mv{i}") for i in range(3)]
        dve_rw, dve_h2, dve_z2 = sem("dve_rw"), sem("dve_h2"), sem("dve_z2")
        dve_top, dve_topi, dve_topf = sem("dve_top"), sem("dve_topi"), sem("dve_topf")
        dve_gap, dve_e1, dve_w1, dve_w2 = sem("dve_gap"), sem("dve_e1"), sem("dve_w1"), sem("dve_w2")
        dve_is = sem("dve_is")
        dve_wab, dve_wt = sem("dve_wab"), sem("dve_wt")
        dve_up, dve_s = sem("dve_up"), sem("dve_s")
        dve_max, dve_sub, dve_rsum, dve_o, dve_y = (
            sem("dve_max"), sem("dve_sub"), sem("dve_rsum"), sem("dve_o"), sem("dve_y"))
        dve_z1, dve_zlo, dve_z2lo = sem("dve_z1"), sem("dve_zlo"), sem("dve_z2lo")
        act_whi, dve_wlo, act_uphi, pool_uplo = sem("act_whi"), sem("dve_wlo"), sem("act_uphi"), sem("pool_uplo")
        pool_zero, pool_kexp = sem("pool_zero"), sem("pool_kexp")
        pool_var = [sem(f"pool_var{i}") for i in range(3)]
        pool_rstd = [sem(f"pool_rstd{i}") for i in range(3)]
        pool_shift1 = sem("pool_shift1")
        N_ZERO = 4

        def row_tile(first, j):
            return bank[first + j // 2][:, (j % 2) * D:(j % 2 + 1) * D]

        def score_bank(g, u):
            return bank[(u + 2) % 4] if g == 0 else bank[2 + u % 2]

        def pT_bank(g, u):
            return bank[6] if g == 0 and u % 2 else bank[4]

        def out_bank(g, u):
            return bank[7] if g == 0 and u % 2 else bank[5]

        def up_first(c, j):
            return 0 if (j % 2 == 1) != (c in (0, G - 1)) else 6

        def up_bank(c, j, m):
            return bank[up_first(c, j) + m]

        def spread_bank(c, j):
            return bank[2 + j] if j < 2 else bank[up_first(c, 2) + j - 2]

        def y_tile(c, j):
            return bank[(4, 2, 5)[j]][:, 0:D] if c >= G - 2 else row_tile(6, j)

        CONV_BANK = [3, 6]
        YT_BANK = [[0, 1], [2, 6]]

        def conv_rows(q, k, h):
            row = 64 * h + 32 * q
            return (y_b[32 * q:32 * q + 32, h * C // 2 + 16 * k:h * C // 2 + 16 * k + 16, :],
                    bank[CONV_BANK[k]][row:row + 32, 0:16 * S].rearrange("p (c t) -> p c t", t=S))

        def yT_rows(q, k):
            return (yT[0:C, 2 * q:2 * q + 2, :, SG // 2 * k:SG // 2 * (k + 1), :].rearrange("c g j s b -> c g j (s b)"),
                    bank[YT_BANK[q][k]][0:C, 0:384].rearrange("c (g j n) -> c g j n", g=2, j=NJ))

        block = ctx.enter_context(nc.Block())

        @block.sync
        def _(sp):
            every_t4 = bass.AP(tensor=taps_in.tensor, offset=taps_in.offset, ap=[[0, T4], [C, TAPS], [1, C]])
            sp.dma_start(taps_rep[:, :], every_t4).then_inc(ld_small, 16)
            for i in range(4):
                part = slice(i % 2 * C // 4, (i % 2 + 1) * C // 4)
                sp.dma_start(x_sb[:, i // 2, part, :, :], x_in[:, i // 2, part, :, :]).then_inc(ld_x[i], 16)
            sp.dma_start(wup[:, :, :], wup_in.rearrange("(c p) n -> p c n", p=128)).then_inc(ld_ffn, 16)
            sp.dma_start(wdown[:, :, :], wdown_in.rearrange("(c p) n -> p c n", p=128)).then_inc(ld_ffn, 16)
            sp.dma_start(gate[:, :, :], gate_in.rearrange("(c p) n -> p c n", p=128)).then_inc(ld_ffn, 16)

            def attend(g):
                sp.wait_ge(act_proj, NP * g + 2 + NJ)
                if g >= 1:
                    sp.wait_ge(v_loaded, 64 * g)
                sp.dma_start(v_scratch.rearrange("j p d -> p j d"), v_sb[:, :, :]).then_inc(v_stored, 16)
                sp.wait_ge(v_stored, 16 * (g + 1))
                sp.wait_ge(pool_zero, N_ZERO)
                if g >= 1:
                    sp.wait_ge(pe_o, Q4 * g)
                rows = v_scratch.rearrange("j p d -> (j p) d").rearrange("(b k) (n c) -> k b n c", k=S, n=4)
                for n in range(4):
                    sp.dma_start(vdiag[n * S:(n + 1) * S, :, n, :, :].rearrange("k b g h -> k b (g h)"),
                                 rows[:, :, n, :]).then_inc(v_loaded, 16)
                for u in range(Q4):
                    sp.wait_ge(dve_o, Q4 * g + u + 1)
                    if g >= 1 and u == 0:
                        sp.wait_ge(r_loaded, 16 * SG * g)
                    sp.dma_start(o_scratch[u], o_sb[:, u, :, :].rearrange("p h n -> p (h n)")).then_inc(o_stored, 16)
                sp.wait_ge(o_stored, 64 * (g + 1))
                if g >= 1:
                    sp.wait_ge(dve_rw, g)
                for k in range(SG):
                    src = bass.AP(tensor=o_scratch.tensor, offset=o_scratch.offset + k * NJ * NH,
                                  ap=[[32 * D, BG], [S * NH, D // NH], [1, NJ * NH]])
                    sp.dma_start(r_sb[k * BG:(k + 1) * BG, :, :, :].rearrange("p d j n -> p d (j n)"), src
                                 ).then_inc(r_loaded, 16)

            def store(c):
                sp.wait_ge(dve_y, NJ * (c + 1))
                dst = out[c * BG:(c + 1) * BG].rearrange("b (s j) d -> s b (j d)", j=NJ)
                sp.dma_start(dst, out_sb[:, :, :].rearrange("p j d -> p (j d)")).then_inc(out_stored, 16)

            for i in range(G + 1):
                if i < G:
                    attend(i)
                if i >= 1:
                    store(i - 1)
            sp.wait_ge(out_stored, 16 * G)

        @block.gpsimd
        def _(pool):
            pool.memset(vdiag[:, :, :, :, :], 0.0).then_inc(pool_zero, 1)
            pool.memset(qT[:, :, TOK:TOK + PAD], 0.0).then_inc(pool_zero, 1)
            pool.memset(neghalf[:, :], -0.5).then_inc(pool_zero, 1)
            pool.wait_ge(pool_zero, N_ZERO - 1)
            pool.wait_ge(ld_const, 32)
            pool.tensor_copy(vdiag[:, :, 4, :, 0:4], keysel.unsqueeze(1).unsqueeze(1).to_broadcast([4 * S, BG, 4, 4])
                             ).then_inc(pool_zero, 1)

            def rsqrt(k, n):
                pool.wait_ge(dve_mv[k], NJ * (n + 1))
                pool.tensor_scalar(vareps[k][:, :], meanvar[k][:, :, 1], EPS, None, ALU.add).then_inc(pool_var[k], 1)
                pool.wait_ge(pool_var[k], n + 1)
                pool.tensor_tensor(rstd[k][:, :], vareps[k][:, :], neghalf[:, :], ALU.pow).then_inc(pool_rstd[k], 1)
                if k == 1 and n >= 1:
                    pool.wait_ge(pool_rstd[k], n + 1)
                    pool.tensor_tensor(shift1[:, :], meanvar[k][:, :, 0], rstd[k][:, :], ALU.mult
                                       ).then_inc(pool_shift1, 1)
                    pool.wait_ge(pool_shift1, 2 * n - 1)
                    pool.tensor_scalar(shift1[:, :], shift1[:, :], -1.0, None, ALU.mult).then_inc(pool_shift1, 1)

            def expand_keys(g, half):
                pool.wait_ge(act_proj, NP * g + half + 1)
                if g >= 1 and half == 0:
                    pool.wait_ge(pe_score, Q4 * g)
                for n in range(K_DVE + K_ACT, 8):
                    pool.tensor_scalar(kexp[:, half, n, :], kT[:, half, :], headsel[:, n:n + 1], None, ALU.mult
                                       ).then_inc(pool_kexp, 1)

            def split_up(k):
                pool.wait_ge(act_uphi, k + 1)
                pool.tensor_tensor(wup_lo[:, k, :], wup[:, k, :], wup_hi[:, k, :], ALU.subtract
                                   ).then_inc(pool_uplo, 1)

            rsqrt(0, 0)
            rsqrt(1, 0)
            for i in range(G):
                expand_keys(i, 0)
                expand_keys(i, 1)
                if i == 0:
                    split_up(0)
                    rsqrt(0, 1)
                    split_up(1)
                    pool.wait_ge(act_uphi, 3)
                    pool.tensor_tensor(gate_lo[:, :, :], gate[:, :, :], gate_hi[:, :, :], ALU.subtract
                                       ).then_inc(pool_uplo, 1)
                if i == 1:
                    rsqrt(2, 0)
                if i + 1 < G:
                    rsqrt(1, i + 1)
                if i + 2 < G:
                    rsqrt(0, i + 2)
                if i >= 1:
                    rsqrt(2, i)

        @block.scalar
        def _(act):
            act.dma_start(band[:, :], band_in).then_inc(ld_small, 16)
            act.dma_start(constf[:, :], constf_in).then_inc(ld_const, 16)
            act.dma_start(constb[:, :], constb_in).then_inc(ld_const, 16)
            act.dma_start(wproj[:, :], wproj_in).then_inc(ld_front, 16)
            act.dma_start(gamma[:, :], gamma_in.partition_broadcast(128)).then_inc(ld_front, 16)
            act.dma_start(beta[:, :], beta_in.partition_broadcast(128)).then_inc(ld_front, 16)
            act.dma_start(wqkv[:, :, :], wqkv_in.rearrange("(c p) n -> p c n", p=128)).then_inc(ld_qkv, 16)
            act.dma_start(wout[:, :, :], wout_in.rearrange("(c p) n -> p c n", p=128)).then_inc(ld_wout, 32)

            act.wait_ge(dve_ones, 1)
            act.activation(egap[:, :], ones[:, 0:NJ], ACT.Exp).then_inc(act_table, 1)

            for k in (0, 2):
                act.wait_ge(pe_toep, k + 1)
                act.copy(toep[:, :, 8 * k:8 * k + 8], bank[k][0:T, :].rearrange("p (t c) -> p c t", t=8)
                         ).then_inc(act_toep, 1)

            def copy_conv(q, k, h):
                act.wait_ge(pe_conv, 2 * q + k + 1)
                act.copy(*conv_rows(q, k, h)).then_inc(act_yb, 1)

            def copy_yT(q, k):
                act.wait_ge(pe_yT, 2 * q + k + 1)
                act.copy(*yT_rows(q, k)).then_inc(act_yT, 1)

            copy_conv(0, 0, 0)
            copy_conv(0, 1, 0)
            copy_yT(0, 0)
            for k in range(2):
                for h in range(2):
                    copy_conv(1, k, h)

            def copy_wsum():
                act.wait_ge(pe_wsum, 1)
                act.copy(wsum[:, :], bank[7][:, 0:D]).then_inc(act_wsum, 1)

            ACT_KEYS = [0, 1, 2, 3, 3, 4]

            def project(g, parts):
                for k in parts:
                    act.wait_ge(pe_proj, NP * g + k + 1)
                    p = bank[k % 2]
                    if k < 2:
                        if g >= 1 and k == 0:
                            act.wait_ge(pool_kexp, 2 * K_POOL * g)
                            act.wait_ge(dve_kexp, 2 * K_DVE * g)
                        ins = act.copy(kT[:, k, :], p[:, 0:TOK])
                    elif k < 2 + NJ:
                        if g >= 1:
                            act.wait_ge(v_stored, 16 * g)
                        ins = act.copy(v_sb[:, k - 2, :], p[:, 0:D])
                    else:
                        if g >= 1:
                            act.wait_ge(pe_score, Q4 * g)
                        ins = act.mul(qT[:, k - 2 - NJ, 0:TOK], p[:, 0:TOK], HD ** -0.5)
                    ins.then_inc(act_proj, 1)
                    if k >= 2:
                        if k == 2:
                            act.wait_ge(ld_const, 32)
                            act.wait_ge(act_proj, NP * g + 2)
                            if g >= 1:
                                act.wait_ge(pe_score, Q4 * g)
                        for m in range(ACT_KEYS[k - 2], ACT_KEYS[k - 1]):
                            half, n = m // K_ACT, K_DVE + m % K_ACT
                            act.activation(kexp[:, half, n, :], kT[:, half, :], ACT.Copy,
                                           scale=headsel[:, n:n + 1]).then_inc(act_kexp, 1)

            def front_norm2(n):
                act.wait_ge(pe_zT, 2 * n)
                act.wait_ge(pool_shift1, 2 * n)
                for j in range(NJ):
                    act.activation(z1[:, j, :], hres[:, NJ * n + j, :], ACT.Identity, bias=shift1[:, j:j + 1],
                                   scale=rstd[1][:, j:j + 1]).then_inc(act_z1, 1)

            def front_zT(n):
                if n >= 1:
                    act.wait_ge(pe_proj, NP * n)
                for k in range(2):
                    act.wait_ge(pe_zT, 2 * n + k + 1)
                    act.copy(zT_hi[:, k, 0:TOK].rearrange("p (b s j) -> p j s b", b=BG, j=NJ),
                             bank[4 + k][:, 0:TOK].rearrange("p (j s b) -> p j s b", j=NJ, s=SG)
                             ).then_inc(act_zT, 1)

            def feed_z2T(c):
                for k in range(2):
                    act.wait_ge(pe_z2T, 2 * c + k + 1)
                    if c >= 1:
                        act.wait_ge(pe_up, 8 * c)
                    act.copy(z2T_hi[:, k, :], bank[6 + k][:, 0:TOK]).then_inc(act_z2T, 1)

            def feed_logit(c):
                act.wait_ge(pe_logit, c + 1)
                act.copy(logitT[:, :], bank[5][0:E, 0:TOK]).then_inc(act_logit, 1)

            def feed_logits(c):
                act.wait_ge(pe_logits, c + 1)
                if c >= 1:
                    act.wait_ge(dve_topi, NJ * c)
                act.copy(logits[:, :, :], bank[5][:, 0:NJ * E].rearrange("p (j e) -> p j e", j=NJ)
                         ).then_inc(act_logits, 1)

            def tanh(c, j):
                act.wait_ge(pe_up, 8 * c + 2 * j + 1)
                if j >= 2:
                    act.wait_ge(dve_up, 8 * c + 2 * j - 3)
                act.activation(th[:, j % 2, :], up_bank(c, j, 0)[:, 0:TOK], ACT.Tanh, scale=0.5).then_inc(act_tanh, 1)

            def exp_gap(c):
                act.wait_ge(dve_gap, c + 1)
                if c == 0:
                    act.wait_ge(act_table, 1)
                act.activation(egap[:, :], gap[:, :], ACT.Exp).then_inc(act_egap, 1)

            def expand_weights(c):
                act.wait_ge(dve_wt, c + 1)
                if c >= 1:
                    act.wait_ge(pe_wbc, NF * c)
                act.copy(wexp[:, :, :, :], wt[:, :, :].unsqueeze(3).to_broadcast([128, NJ, E, R])
                         ).then_inc(act_wexp, 1)

            def exp_scores(g, u):
                act.wait_ge(dve_sub, Q4 * g + u + 1)
                act.activation(probs[:, u, :], probs[:, u, :], ACT.Exp).then_inc(act_exp, 1)

            def evac_pT(g, u):
                act.wait_ge(pe_pT, Q4 * g + u + 1)
                if g >= 1 and u == 0:
                    act.wait_ge(pe_o, Q4 * g)
                act.copy(pT[:, u, :, :], pT_bank(g, u)[0:4 * S, :].rearrange("p (n q) -> p n q", n=4)
                         ).then_inc(act_pT, 1)

            copy_wsum()
            copy_yT(1, 0)
            copy_yT(1, 1)
            act.wait_ge(ld_qkv, 16)
            for k in range(2):
                act.copy(wqkv_hi[:, k, :], wqkv[:, k, :]).then_inc(act_whi, 1)
            act.wait_ge(ld_ffn, 48)
            for k in range(2):
                act.copy(wup_hi[:, k, :], wup[:, k, :]).then_inc(act_uphi, 1)
            act.copy(gate_hi[:, :, :], gate[:, :, :]).then_inc(act_uphi, 1)
            front_zT(0)
            for i in range(G + 1):
                attend = i < G
                if i == 0:
                    project(0, range(2 + NJ))
                    project(0, range(2 + NJ, NP))
                    exp_scores(0, 0)
                    exp_scores(0, 1)
                    evac_pT(0, 0)
                    exp_scores(0, 2)
                    evac_pT(0, 1)
                    exp_scores(0, 3)
                    evac_pT(0, 2)
                    evac_pT(0, 3)
                    front_norm2(1)
                    front_zT(1)
                    continue
                if i == 1:
                    project(1, range(2 + NJ))
                    project(1, range(2 + NJ, NP))
                    feed_z2T(0)
                    exp_scores(1, 0)
                    exp_scores(1, 1)
                    tanh(0, 0)
                elif attend:
                    project(i, range(2 + NJ))
                    feed_z2T(i - 1)
                    project(i, range(2 + NJ, NP))
                    tanh(i - 1, 0)
                    exp_scores(i, 0)
                    exp_scores(i, 1)
                if i == G:
                    feed_z2T(i - 1)
                    tanh(i - 1, 0)
                    feed_logit(i - 1)
                    feed_logits(i - 1)
                    tanh(i - 1, 1)
                    exp_gap(i - 1)
                    tanh(i - 1, 2)
                    expand_weights(i - 1)
                    tanh(i - 1, 3)
                elif i == G - 1:
                    feed_logit(i - 1)
                    evac_pT(i, 0)
                    feed_logits(i - 1)
                    tanh(i - 1, 1)
                    exp_scores(i, 2)
                    evac_pT(i, 1)
                    exp_gap(i - 1)
                    exp_scores(i, 3)
                    evac_pT(i, 2)
                    evac_pT(i, 3)
                    expand_weights(i - 1)
                    tanh(i - 1, 2)
                    tanh(i - 1, 3)
                else:
                    feed_logit(i - 1)
                    evac_pT(i, 0)
                    tanh(i - 1, 1)
                    feed_logits(i - 1)
                    exp_scores(i, 2)
                    evac_pT(i, 1)
                    exp_gap(i - 1)
                    exp_scores(i, 3)
                    tanh(i - 1, 2)
                    evac_pT(i, 2)
                    front_norm2(i + 1)
                    evac_pT(i, 3)
                    expand_weights(i - 1)
                    tanh(i - 1, 3)
                    front_zT(i + 1)

        @block.vector
        def _(dve):
            dve.memset(ones[:, :], 1.0).then_inc(dve_ones, 1)
            dve.memset(taps[:, :, :], 0.0).then_inc(dve_ones, 1)
            dve.memset(yT[C:C + 1, :, :, :, :], 1.0).then_inc(dve_ones, 1)

            dve.wait_ge(ld_small, 32)
            dve.wait_ge(dve_ones, 2)
            for k in range(T4):
                rows = slice(k * TAPS, (k + 1) * TAPS)
                dve.tensor_copy(taps[rows, k, :], taps_rep[rows, :]).then_inc(dve_taps, 1)
            dve.wait_ge(pe_toep, 2)
            dve.tensor_copy(toep[:, :, 8:16], bank[1][0:T, :].rearrange("p (t c) -> p c t", t=8)).then_inc(dve_toep, 1)
            for k in range(2):
                dve.wait_ge(pe_conv, k + 1)
                dve.tensor_copy(*conv_rows(0, k, 1)).then_inc(dve_yb, 1)
            dve.wait_ge(pe_yT, 2)
            dve.tensor_copy(*yT_rows(0, 1)).then_inc(dve_yT, 1)

            def layer_stats(k, n, src):
                for j in range(NJ):
                    dve.bn_stats(stats[k][:, j, :], src(j)).then_inc(dve_stats[k], 1)
                for j in range(NJ):
                    dve.wait_ge(dve_stats[k], NJ * n + j + 1)
                    dve.bn_aggr(meanvar[k][:, j, :], stats[k][:, j, :]).then_inc(dve_mv[k], 1)

            def normalise(k, n, dst, src, done):
                dve.wait_ge(pool_rstd[k], n + 1)
                for j in range(NJ):
                    dve.tensor_scalar(dst(j), src(j), meanvar[k][:, j, 0:1], rstd[k][:, j:j + 1],
                                      ALU.subtract, ALU.mult).then_inc(done, 1)

            def front_stats(n):
                dve.wait_ge(pe_h, NJ * (n + 1))
                layer_stats(0, n, lambda j: row_tile(4, j))
                dve.wait_ge(dve_mv[0], NJ * (n + 1))
                for j in range(NJ):
                    dve.scalar_tensor_tensor(out=h_cent[:, j, :], in0=row_tile(4, j), scalar=meanvar[0][:, j, 0:1],
                                             in1=gamma[:, :], op0=ALU.subtract, op1=ALU.mult).then_inc(dve_cent, 1)

            def front_affine(n):
                dve.wait_ge(pool_rstd[0], n + 1)
                dve.wait_ge(dve_cent, NJ * (n + 1))
                for j in range(NJ):
                    dve.scalar_tensor_tensor(out=hres[:, NJ * n + j, :], in0=h_cent[:, j, :],
                                             scalar=rstd[0][:, j:j + 1], in1=beta[:, :], op0=ALU.mult, op1=ALU.add
                                             ).then_inc(dve_h1, 1)
                dve.wait_ge(dve_h1, NJ * (n + 1))
                layer_stats(1, n, lambda j: hres[:, NJ * n + j, :])

            def front_zlo(n):
                for k in range(2):
                    dve.wait_ge(act_zT, 2 * n + k + 1)
                    dve.tensor_tensor(zT_lo[:, k, 0:TOK].rearrange("p (b s j) -> p j s b", b=BG, j=NJ),
                                      bank[4 + k][:, 0:TOK].rearrange("p (j s b) -> p j s b", j=NJ, s=SG),
                                      zT_hi[:, k, 0:TOK].rearrange("p (b s j) -> p j s b", b=BG, j=NJ),
                                      ALU.subtract).then_inc(dve_zlo, 1)

            def feed_z2lo(c):
                for k in range(2):
                    dve.wait_ge(act_z2T, 2 * c + k + 1)
                    dve.tensor_tensor(z2T_lo[:, k, :], bank[6 + k][:, 0:TOK], z2T_hi[:, k, :], ALU.subtract
                                      ).then_inc(dve_z2lo, 1)

            def expand_keys(g, half):
                dve.wait_ge(act_proj, NP * g + half + 1)
                if g >= 1 and half == 0:
                    dve.wait_ge(pe_score, Q4 * g)
                for n in range(K_DVE):
                    dve.tensor_scalar(kexp[:, half, n, :], kT[:, half, :], headsel[:, n:n + 1], None, ALU.mult
                                      ).then_inc(dve_kexp, 1)

            def feed_residual(c):
                dve.wait_ge(r_loaded, 16 * SG * (c + 1))
                dve.tensor_tensor(rw[:, :, :].rearrange("p j (n d) -> p j n d", n=NH),
                                  r_sb[:, :, :, :].rearrange("p d j n -> p j n d"),
                                  wsum[:, :].rearrange("p (n d) -> p n d", n=NH).unsqueeze(1)
                                  .to_broadcast([128, NJ, NH, D // NH]), ALU.mult).then_inc(dve_rw, 1)
                dve.wait_ge(dve_rw, c + 1)
                h = hres[:, NJ * c:NJ * c + NJ, :]
                dve.tensor_tensor(h, h, rw[:, :, :], ALU.add).then_inc(dve_h2, 1)
                dve.wait_ge(dve_h2, c + 1)
                layer_stats(2, c, lambda j: hres[:, NJ * c + j, :])

            def feed_norm(c):
                if c >= 1:
                    dve.wait_ge(pe_z2T, 2 * c)
                normalise(2, c, lambda j: z2[:, j, :], lambda j: hres[:, NJ * c + j, :], dve_z2)

            def feed_gate(c):
                dve.wait_ge(act_logits, c + 1)
                for j in range(NJ):
                    dve.max(top[:, j, :], logits[:, j, :]).then_inc(dve_top, 1)
                dve.wait_ge(dve_top, NJ * (c + 1))
                dve.tensor_tensor(gap[:, :], top[:, :, 1], top[:, :, 0], ALU.subtract).then_inc(dve_gap, 1)
                for j in range(NJ):
                    dve.max_index(topi[:, j, :], top[:, j, :], logits[:, j, :]).then_inc(dve_topi, 1)
                dve.wait_ge(dve_topi, NJ * (c + 1))
                dve.tensor_copy(topf[:, :, :], topi[:, :, :]).then_inc(dve_topf, 1)

            def feed_weights(c):
                dve.wait_ge(act_egap, c + 1)
                dve.tensor_scalar(egap1[:, :], egap[:, :], 1.0, 2.0, ALU.add, ALU.mult).then_inc(dve_e1, 1)
                dve.wait_ge(dve_e1, c + 1)
                dve.reciprocal(w_first[:, :], egap1[:, :]).then_inc(dve_w1, 1)
                dve.wait_ge(dve_w1, c + 1)
                dve.tensor_tensor(w_second[:, :], egap[:, :], w_first[:, :], ALU.mult).then_inc(dve_w2, 1)
                dve.wait_ge(dve_topf, c + 1)
                dve.wait_ge(dve_w2, c + 1)
                every = lambda ap: ap.unsqueeze(2).to_broadcast([128, NJ, E])
                number = iota.unsqueeze(1).to_broadcast([128, NJ, E])
                dve.tensor_tensor(is_a[:, :, :], number, every(topf[:, :, 0]), ALU.is_equal).then_inc(dve_is, 1)
                dve.tensor_tensor(is_b[:, :, :], number, every(topf[:, :, 1]), ALU.is_equal).then_inc(dve_is, 1)
                dve.wait_ge(dve_is, 2 * c + 1)
                dve.tensor_tensor(wa[:, :, :], is_a[:, :, :], every(w_first[:, :]), ALU.mult).then_inc(dve_wab, 1)
                dve.wait_ge(dve_is, 2 * c + 2)
                dve.tensor_tensor(wb[:, :, :], is_b[:, :, :], every(w_second[:, :]), ALU.mult).then_inc(dve_wab, 1)
                dve.wait_ge(dve_wab, 2 * (c + 1))
                if c >= 1:
                    dve.wait_ge(act_wexp, c)
                dve.tensor_tensor(wt[:, :, :], wa[:, :, :], wb[:, :, :], ALU.add).then_inc(dve_wt, 1)

            def feed_gated(c, j):
                dve.wait_ge(act_tanh, NF * c + j + 1)
                dve.scalar_tensor_tensor(out=ug[:, j % 2, :], in0=th[:, j % 2, :], scalar=1.0,
                                         in1=up_bank(c, j, 0)[:, 0:TOK], op0=ALU.add, op1=ALU.mult).then_inc(dve_up, 1)
                dve.wait_ge(dve_up, 8 * c + 2 * j + 1)
                dve.wait_ge(pe_up, 8 * c + 2 * j + 2)
                if c >= 1:
                    dve.wait_ge(pe_y, NJ * c)
                dve.tensor_tensor(sT[:, j, :], ug[:, j % 2, :], up_bank(c, j, 1)[:, 0:TOK], ALU.mult
                                  ).then_inc(dve_up, 1)

            def feed_scale(c, j):
                dve.wait_ge(pe_wbc, NF * c + j + 1)
                dve.wait_ge(dve_up, 8 * c + 2 * j + 2)
                dve.tensor_tensor(sT[:, j, :], sT[:, j, :], spread_bank(c, j)[:, 0:TOK], ALU.mult).then_inc(dve_s, 1)

            def feed_out(c):
                if c >= 1:
                    dve.wait_ge(out_stored, 16 * c)
                for n, j in enumerate((2, 0, 1)):
                    if c >= G - 2:
                        dve.wait_ge(pe_y, NJ * c + n + 1)
                    else:
                        dve.wait_ge(pe_y, NJ * c + (1 if j == 2 else NJ))
                    dve.tensor_tensor(out_sb[:, j, :], y_tile(c, j), hres[:, NJ * c + j, :], ALU.add
                                      ).then_inc(dve_y, 1)

            def shift_scores(g, u):
                if g >= 1 and u == 0:
                    dve.wait_ge(pe_pT, Q4 * g)
                sc = score_bank(g, u)[:, 0:NH * S].rearrange("p (n k) -> p n k", n=NH)
                dve.wait_ge(pe_score, Q4 * g + u + 1)
                dve.tensor_reduce(smax[:, u, :], sc, X, ALU.max).then_inc(dve_max, 1)
                dve.wait_ge(dve_max, Q4 * g + u + 1)
                dve.tensor_tensor(probs[:, u, :].rearrange("p (n k) -> p n k", n=NH), sc,
                                  smax[:, u, :].unsqueeze(2).to_broadcast([128, NH, S]), ALU.subtract
                                  ).then_inc(dve_sub, 1)

            def scale_out(g, u):
                dve.wait_ge(pe_o, Q4 * g + u + 1)
                o = out_bank(g, u)[:, 0:4 * OW].rearrange("p (n c) -> p n c", n=4)
                dve.reciprocal(rsum[:, u, :, :], o[:, :, 4 * HD:4 * HD + 4]).then_inc(dve_rsum, 1)
                dve.wait_ge(dve_rsum, Q4 * g + u + 1)
                if g >= 1 and u == 0:
                    dve.wait_ge(o_stored, 64 * g)
                dve.tensor_tensor(o_sb[:, u, :, :].rearrange("p h (n m) -> p n m h", n=4),
                                  o[:, :, 0:4 * HD].rearrange("p n (m h) -> p n m h", m=4),
                                  rsum[:, u, :, :].unsqueeze(3).to_broadcast([128, 4, 4, HD]), ALU.mult
                                  ).then_inc(dve_o, 1)

            dve.wait_ge(ld_front, 48)
            front_stats(0)
            front_affine(0)
            for k in range(2):
                dve.wait_ge(act_whi, k + 1)
                dve.tensor_tensor(wqkv_lo[:, k, :], wqkv[:, k, :], wqkv_hi[:, k, :], ALU.subtract).then_inc(dve_wlo, 1)
                if k == 0:
                    normalise(1, 0, lambda j: z1[:, j, :], lambda j: hres[:, j, :], dve_z1)
            front_zlo(0)
            dve.wait_ge(ld_const, 32)
            for i in range(G + 1):
                attend = i < G
                if i == 0:
                    expand_keys(0, 1)
                    expand_keys(0, 0)
                    front_stats(1)
                    shift_scores(0, 0)
                    shift_scores(0, 1)
                    shift_scores(0, 2)
                    shift_scores(0, 3)
                    front_affine(1)
                    scale_out(0, 0)
                    scale_out(0, 1)
                    scale_out(0, 2)
                    scale_out(0, 3)
                    front_zlo(1)
                    front_stats(2)
                    continue
                if i == 1:
                    dve.wait_ge(act_wsum, 1)
                    expand_keys(1, 0)
                    expand_keys(1, 1)
                    feed_residual(0)
                    feed_norm(0)
                    shift_scores(1, 0)
                    feed_z2lo(0)
                    shift_scores(1, 1)
                elif attend:
                    expand_keys(i, 0)
                    feed_z2lo(i - 1)
                    expand_keys(i, 1)
                    shift_scores(i, 0)
                    shift_scores(i, 1)
                if i == G:
                    feed_z2lo(i - 1)
                    feed_gated(i - 1, 0)
                    feed_gate(i - 1)
                    feed_gated(i - 1, 1)
                    feed_weights(i - 1)
                    feed_gated(i - 1, 2)
                    feed_scale(i - 1, 0)
                    feed_scale(i - 1, 1)
                    feed_scale(i - 1, 2)
                    feed_gated(i - 1, 3)
                    feed_scale(i - 1, 3)
                    feed_out(i - 1)
                elif i == G - 1:
                    feed_gated(i - 1, 0)
                    shift_scores(i, 2)
                    feed_gate(i - 1)
                    scale_out(i, 0)
                    shift_scores(i, 3)
                    feed_gated(i - 1, 1)
                    scale_out(i, 1)
                    scale_out(i, 2)
                    feed_weights(i - 1)
                    scale_out(i, 3)
                    feed_gated(i - 1, 2)
                    feed_scale(i - 1, 0)
                    feed_gated(i - 1, 3)
                    feed_scale(i - 1, 1)
                    feed_scale(i - 1, 2)
                    feed_scale(i - 1, 3)
                    feed_residual(i)
                    feed_out(i - 1)
                    feed_norm(i)
                else:
                    front_affine(i + 1)
                    feed_gated(i - 1, 0)
                    shift_scores(i, 2)
                    feed_gate(i - 1)
                    feed_gated(i - 1, 1)
                    scale_out(i, 0)
                    shift_scores(i, 3)
                    feed_weights(i - 1)
                    scale_out(i, 1)
                    feed_gated(i - 1, 2)
                    scale_out(i, 2)
                    scale_out(i, 3)
                    feed_gated(i - 1, 3)
                    feed_scale(i - 1, 0)
                    feed_scale(i - 1, 1)
                    feed_scale(i - 1, 2)
                    feed_scale(i - 1, 3)
                    front_zlo(i + 1)
                    if i + 2 < G:
                        front_stats(i + 2)
                    feed_residual(i)
                    feed_out(i - 1)
                    feed_norm(i)

        @block.tensor
        def _(pe):
            mm = pe.matmul

            def keep_warm(n):
                for k in range(n):
                    mm(bank[3][:, 0:128], ones[:, :], ones[:, :], start=True, stop=True)

            pe.wait_ge(dve_ones, 1)
            keep_warm(4)
            pe.wait_ge(ld_small, 32)
            pe.wait_ge(dve_taps, T4)
            for k in range(S // T4):
                shift = SPAN - STRIDE * T4 * k
                last = mm(bank[k // 2][0:T, (k % 2) * T4 * C:(k % 2 + 1) * T4 * C], band[:, shift:shift + T],
                          taps[:, :, :].rearrange("j t c -> j (t c)"), start=True, stop=True)
                if k % 2:
                    last.then_inc(pe_toep, 1)
            keep_warm(2)
            pe.wait_ge(act_toep, 2)
            pe.wait_ge(dve_toep, 1)

            def convolve(q, k):
                pe.wait_ge(ld_x[2 * q + k], 16)
                for c in range(16 * k, 16 * k + 16):
                    for h in range(2):
                        row = 64 * h + 32 * q
                        last = mm(bank[CONV_BANK[k]][row:row + 32, (c % 16) * S:(c % 16 + 1) * S],
                                  x_sb[:, q, c, h, :], toep[:, h * C // 2 + c, :],
                                  start=True, stop=True, tile_position=(0, row))
                last.then_inc(pe_conv, 1)

            def transpose_y(q):
                pe.wait_ge(ld_const, 32)
                if q == 0:
                    pe.wait_ge(act_yb, 2)
                    pe.wait_ge(dve_yb, 2)
                else:
                    pe.wait_ge(act_yb, 6)
                for k in range(2):
                    for s in range(SG // 2):
                        for j in range(NJ):
                            dst = bank[YT_BANK[q][k]][0:C, 0:384].rearrange("c (g j s b) -> c g j s b", g=2, j=NJ,
                                                                            b=BG)
                            pos = NJ * (SG // 2 * k + s) + j
                            last = pe.transpose(dst[:, :, j, s, :], y_b[32 * q:32 * q + 32, :, pos],
                                                ident[32 * q:32 * q + 32, 32 * q:32 * q + 32])
                    last.then_inc(pe_yT, 1)

            def sum_wout():
                for k in range(2):
                    last = mm(bank[7][:, 0:D], ones[:, :], wout[:, k, :], start=(k == 0), stop=(k == 1))
                last.then_inc(pe_wsum, 1)

            def front_h(n):
                if n == 0:
                    pe.wait_ge(act_yT, 1)
                    pe.wait_ge(dve_yT, 1)
                    pe.wait_ge(dve_ones, 3)
                elif n == 2:
                    pe.wait_ge(act_yT, 3)
                if n >= 1:
                    pe.wait_ge(dve_zlo, 2 * n)
                for j in range(NJ):
                    mm(row_tile(4, j), yT[:, n, j, :, :].rearrange("c s b -> c (s b)"), wproj[:, :],
                       start=True, stop=True).then_inc(pe_h, 1)

            def front_zT(n):
                if n >= 1:
                    pe.wait_ge(act_pT, Q4 * n)
                    pe.wait_ge(dve_o, Q4 * n)
                else:
                    pe.wait_ge(dve_cent, NJ)
                for j in range(NJ):
                    if n == 0:
                        pe.wait_ge(dve_z1, j + 1)
                    else:
                        pe.wait_ge(act_z1, NJ * (n - 1) + j + 1)
                    for k in range(2):
                        last = pe.transpose(bank[4 + k][:, 128 * j:128 * j + 128], z1[:, j, 128 * k:128 * k + 128],
                                            ident)
                        if j == NJ - 1:
                            last.then_inc(pe_zT, 1)

            SPLIT = [(0, 0, 0), (1, 0, 0), (0, 0, 1), (1, 0, 1), (0, 1, 0), (0, 1, 1)]

            def project(g, parts):
                pe.wait_ge(dve_wlo, 2)
                for k in parts:
                    if k >= 2:
                        pe.wait_ge(act_proj, NP * g + k - 1)
                    elif g == 1:
                        pe.wait_ge(dve_sub, 3 + k)
                    elif g == 2:
                        pe.wait_ge(dve_s, NF - 1 + k)
                    elif g > 2:
                        pe.wait_ge(dve_up, 8 * (g - 1) - 1 + k)
                    for step, (wlo, zlo, d) in enumerate(SPLIT):
                        if k == 0 and zlo:
                            pe.wait_ge(dve_zlo, 2 * g + d + 1)
                        elif k == 0 and not wlo:
                            pe.wait_ge(act_zT, 2 * g + d + 1)
                        w, z = (wqkv_hi, wqkv_lo)[wlo], (zT_hi, zT_lo)[zlo]
                        if 2 <= k < 2 + NJ:
                            last = mm(bank[k % 2][:, 0:D], z[:, d, (k - 2) * 128:(k - 1) * 128],
                                      w[:, d, 2 * D:3 * D], start=(step == 0), stop=(step == 5))
                        else:
                            col = 128 * k if k < 2 else D + 128 * (k - 2 - NJ)
                            last = mm(bank[k % 2][:, 0:TOK], w[:, d, col:col + 128], z[:, d, :],
                                      start=(step == 0), stop=(step == 5))
                    last.then_inc(pe_proj, 1)

            def scores(g, u):
                if u == 0:
                    pe.wait_ge(dve_kexp, 2 * K_DVE * (g + 1))
                    pe.wait_ge(act_kexp, 2 * K_ACT * (g + 1))
                    pe.wait_ge(pool_kexp, 2 * K_POOL * (g + 1))
                    pe.wait_ge(pool_zero, N_ZERO)
                    pe.wait_ge(act_proj, NP * g + NP)
                if g >= 1 and u >= 2:
                    pe.wait_ge(dve_sub, Q4 * g + u - 1)
                elif g >= 2:
                    pe.wait_ge(dve_s, NF * (g - 2) + 1 + u)
                elif g == 1:
                    pe.wait_ge(dve_sub, u + 1)
                mm(score_bank(g, u)[:, 0:NH * S], identb, causal, start=True, stop=True)
                for k in range(2):
                    for b4 in range(4):
                        b = 4 * u + b4
                        last = mm(score_bank(g, u)[32 * b4:32 * b4 + 32, 192 * k:192 * k + 192],
                                  qT[:, k, b * S:b * S + 32], kexp[:, k, :, b * S:(b + 1) * S],
                                  start=False, stop=True, skip_group_check=True, tile_position=(0, 32 * b4))
                last.then_inc(pe_score, 1)

            def transpose_probs(g, u):
                pe.wait_ge(act_exp, Q4 * g + u + 1)
                if g == 0 and u == 1:
                    pe.wait_ge(act_yT, 3)
                elif g == 0 and u >= 2:
                    pe.wait_ge(act_pT, u - 1)
                elif u >= 1:
                    pe.wait_ge(act_pT, Q4 * g + u)
                elif g + 1 < G:
                    pe.wait_ge(dve_cent, NJ * (g + 2))
                else:
                    pe.wait_ge(dve_zlo, 2 * (g + 1))
                for n in range(4):
                    last = pe.transpose(pT_bank(g, u)[0:4 * S, 128 * n:128 * n + 128],
                                        probs[:, u, 96 * n:96 * n + 96], ident)
                last.then_inc(pe_pT, 1)

            def attend_out(g, u):
                pe.wait_ge(act_pT, Q4 * g + u + 1)
                pe.wait_ge(v_loaded, 64 * (g + 1))
                if g == 0 and u == 1:
                    pe.wait_ge(act_wsum, 1)
                elif g == 0 and u >= 2:
                    pe.wait_ge(dve_o, u - 1)
                elif u >= 1:
                    pe.wait_ge(dve_o, Q4 * g + u)
                elif g >= 1:
                    pe.wait_ge(act_logits, g)
                else:
                    pe.wait_ge(dve_cent, 2 * NJ)
                for n in range(4):
                    for b4 in range(4):
                        last = mm(out_bank(g, u)[32 * b4:32 * b4 + 32, OW * n:OW * (n + 1)],
                                  pT[:, u, n, 32 * b4:32 * b4 + 32], vdiag[:, 4 * u + b4, :, n, :],
                                  start=True, stop=True, tile_position=(0, 32 * b4))
                last.then_inc(pe_o, 1)

            def feed_z2T(c):
                if c >= 1:
                    pe.wait_ge(dve_y, NJ * c)
                else:
                    pe.wait_ge(act_pT, Q4)
                    pe.wait_ge(dve_o, Q4)
                for j in range(NJ):
                    pe.wait_ge(dve_z2, NJ * c + j + 1)
                    for k in range(2):
                        last = pe.transpose(bank[6 + k][:, 128 * j:128 * j + 128], z2[:, j, 128 * k:128 * k + 128],
                                            ident)
                        if j == NJ - 1:
                            last.then_inc(pe_z2T, 1)

            def feed_logit(c):
                pe.wait_ge(pool_uplo, 3)
                pe.wait_ge(dve_z2lo, 2 * (c + 1))
                if c + 2 < G:
                    pe.wait_ge(dve_cent, NJ * (c + 3))
                elif c + 1 < G:
                    pe.wait_ge(dve_zlo, 2 * (c + 2))
                else:
                    pe.wait_ge(dve_o, Q4 * G)
                for step, (wlo, zlo, k) in enumerate(SPLIT):
                    last = mm(bank[5][0:E, 0:TOK], (gate_hi, gate_lo)[wlo][:, k, :], (z2T_hi, z2T_lo)[zlo][:, k, :],
                              start=(step == 0), stop=(step == 5))
                last.then_inc(pe_logit, 1)

            def feed_logits(c):
                pe.wait_ge(act_logit, c + 1)
                for j in range(NJ):
                    last = pe.transpose(bank[5][:, E * j:E * j + E], logitT[:, 128 * j:128 * j + 128],
                                        ident[0:E, 0:E])
                last.then_inc(pe_logits, 1)

            def feed_up(c, j, parts=(0, 1)):
                for m in parts:
                    if j >= 2:
                        pe.wait_ge(dve_up, 8 * c + 2 * (j - 2) + m + 1)
                    elif up_first(c, j) == 0 and c + 1 < G:
                        pe.wait_ge(act_proj, NP * (c + 2) - m)
                    elif up_first(c, j) == 0:
                        pe.wait_ge(dve_up, 8 * c - 1 + m)
                    else:
                        pe.wait_ge(dve_z2lo, 2 * c + m + 1)
                    if j == 0:
                        pe.wait_ge(pool_uplo, 3)
                    col = m * E * R + 128 * j
                    for step, (wlo, zlo, k) in enumerate(SPLIT):
                        if j == 0 and zlo:
                            pe.wait_ge(dve_z2lo, 2 * c + k + 1)
                        elif j == 0 and not wlo:
                            pe.wait_ge(act_z2T, 2 * c + k + 1)
                        last = mm(up_bank(c, j, m)[:, 0:TOK], (wup_hi, wup_lo)[wlo][:, k, col:col + 128],
                                  (z2T_hi, z2T_lo)[zlo][:, k, :], start=(step == 0), stop=(step == 5))
                    last.then_inc(pe_up, 1)

            def feed_spread(c, j):
                pe.wait_ge(act_wexp, c + 1)
                if j >= 2:
                    pe.wait_ge(dve_up, 8 * c + 6)
                elif c + 1 < G:
                    pe.wait_ge(dve_sub, Q4 * (c + 1) + 3 + j)
                else:
                    pe.wait_ge(dve_s, NF * (c - 1) + 1 + j)
                for m in range(NJ):
                    last = pe.transpose(spread_bank(c, j)[:, 128 * m:128 * m + 128],
                                        wexp[:, m, 2 * j:2 * j + 2, :].rearrange("p e r -> p (e r)"), ident)
                last.then_inc(pe_wbc, 1)

            def feed_down(c, parts):
                pe.wait_ge(dve_s, NF * (c + 1))
                for j in parts:
                    for k in range(NF):
                        last = mm(y_tile(c, j), sT[:, k, 128 * j:128 * j + 128], wdown[:, k, :],
                                  start=(k == 0), stop=(k == NF - 1))
                    last.then_inc(pe_y, 1)

            def feed_down_late(c):
                pe.wait_ge(act_pT, Q4 * G)
                pe.wait_ge(dve_o, Q4 * G)
                pe.wait_ge(act_logits, c + 1)
                for k in range(NF):
                    pe.wait_ge(dve_s, NF * c + k + 1)
                    for j in (2, 0, 1):
                        last = mm(y_tile(c, j), sT[:, k, 128 * j:128 * j + 128], wdown[:, k, :],
                                  start=(k == 0), stop=(k == NF - 1))
                        if k == NF - 1:
                            last.then_inc(pe_y, 1)

            convolve(0, 0)
            convolve(0, 1)
            transpose_y(0)
            convolve(1, 0)
            pe.wait_ge(ld_front, 48)
            front_h(0)
            convolve(1, 1)
            pe.wait_ge(ld_wout, 32)
            sum_wout()
            transpose_y(1)
            keep_warm(8)
            front_zT(0)
            pe.wait_ge(ld_qkv, 16)
            for i in range(G + 1):
                attend = i < G
                if i == 0:
                    project(0, range(2 + NJ))
                    front_h(1)
                    project(0, range(2 + NJ, NP))
                    scores(0, 0)
                    scores(0, 1)
                    scores(0, 2)
                    scores(0, 3)
                    transpose_probs(0, 0)
                    attend_out(0, 0)
                    transpose_probs(0, 1)
                    transpose_probs(0, 2)
                    transpose_probs(0, 3)
                    attend_out(0, 1)
                    attend_out(0, 2)
                    attend_out(0, 3)
                    front_zT(1)
                    front_h(2)
                    continue
                if i == 1:
                    pe.wait_ge(ld_ffn, 48)
                    project(1, range(2 + NJ))
                    project(1, range(2 + NJ, NP))
                    scores(1, 0)
                    scores(1, 1)
                    feed_z2T(0)
                    feed_up(0, 0, [0])
                    feed_up(0, 0, [1])
                elif attend:
                    project(i, range(2 + NJ))
                    feed_z2T(i - 1)
                    project(i, range(2 + NJ, NP))
                    feed_up(i - 1, 0, [0])
                    feed_up(i - 1, 0, [1])
                    scores(i, 0)
                    scores(i, 1)
                if i == G:
                    keep_warm(12)
                    feed_z2T(i - 1)
                    feed_up(i - 1, 0, [0])
                    feed_up(i - 1, 0, [1])
                    feed_logit(i - 1)
                    feed_up(i - 1, 1, [0])
                    feed_logits(i - 1)
                    feed_up(i - 1, 1, [1])
                    feed_up(i - 1, 2, [0])
                    feed_up(i - 1, 2, [1])
                    feed_up(i - 1, 3, [0])
                    feed_up(i - 1, 3, [1])
                    feed_spread(i - 1, 0)
                    feed_spread(i - 1, 1)
                    feed_spread(i - 1, 2)
                    feed_spread(i - 1, 3)
                    feed_down_late(i - 1)
                elif i == G - 1:
                    feed_logit(i - 1)
                    transpose_probs(i, 0)
                    scores(i, 2)
                    feed_logits(i - 1)
                    feed_up(i - 1, 1, [0])
                    attend_out(i, 0)
                    scores(i, 3)
                    transpose_probs(i, 1)
                    feed_up(i - 1, 1, [1])
                    attend_out(i, 1)
                    transpose_probs(i, 2)
                    attend_out(i, 2)
                    transpose_probs(i, 3)
                    attend_out(i, 3)
                    feed_up(i - 1, 2, [0])
                    feed_up(i - 1, 2, [1])
                    feed_up(i - 1, 3, [0])
                    feed_spread(i - 1, 0)
                    feed_up(i - 1, 3, [1])
                    feed_spread(i - 1, 1)
                    feed_spread(i - 1, 2)
                    feed_spread(i - 1, 3)
                    feed_down_late(i - 1)
                else:
                    feed_logit(i - 1)
                    feed_up(i - 1, 1, [0])
                    transpose_probs(i, 0)
                    scores(i, 2)
                    feed_up(i - 1, 1, [1])
                    feed_logits(i - 1)
                    attend_out(i, 0)
                    transpose_probs(i, 1)
                    scores(i, 3)
                    transpose_probs(i, 2)
                    feed_up(i - 1, 2, [0])
                    attend_out(i, 1)
                    feed_up(i - 1, 2, [1])
                    transpose_probs(i, 3)
                    attend_out(i, 2)
                    feed_up(i - 1, 3, [0])
                    attend_out(i, 3)
                    feed_up(i - 1, 3, [1])
                    feed_spread(i - 1, 0)
                    feed_spread(i - 1, 1)
                    feed_spread(i - 1, 2)
                    feed_spread(i - 1, 3)
                    front_zT(i + 1)
                    feed_down(i - 1, [2])
                    if i + 2 < G:
                        front_h(i + 2)
                    feed_down(i - 1, [0, 1])


def shape_constants(np):
    size = 2 * GPAD + 1
    t = np.arange(size, dtype=np.float32) - np.float32((size - 1) / 2)
    g = np.exp(-t ** 2 / np.float32(2.0 * 2.0 ** 2)).astype(np.float32)
    g = (g / g.sum(dtype=np.float32)).astype(np.float32)
    band = np.zeros((T4 * TAPS, T + SPAN), np.float32)
    for k in range(T4):
        for j in range(TAPS):
            for i in range(size):
                v = SPAN - GPAD + STRIDE * k + j + i
                if 0 <= v < T + SPAN:
                    band[k * TAPS + j, v] = g[i]
    constf = np.zeros((128, 148), np.float32)
    constf[:, 0:128] = np.eye(128)
    for p in range(128):
        constf[p, 128 + p // HD] = 1.0
    constf[:, 136:144] = np.arange(8)
    for p in range(4 * S):
        constf[p, 144 + p // S] = 1.0
    from concourse import mybir as mb
    constb = np.zeros((128, 128 + NH * S), mb.dt.np(mb.dt.bfloat16))
    constb[:, 0:128] = np.eye(128)
    for p in range(128):
        q = p % 32
        if q < S:
            for n in range(NH):
                constb[p, 128 + n * S + q + 1:128 + (n + 1) * S] = -1e10
    return band, constf, constb


def kernel(**inputs):
    import numpy as np
    import concourse.bacc as bacc
    from concourse import mybir as mb
    from concourse.bass_utils import run_bass_kernel_spmd as run

    a = {k: np.asarray(v) for k, v in inputs.items()}
    band, constf, constb = shape_constants(np)
    wqkv = a["L0_attn_W_qkv"].reshape(NH, D, 3, HD)
    cols = lambda w: w.transpose(1, 0, 2).reshape(D, NH * HD)
    wv = wqkv[:, :, 2].reshape(4, 4, D, HD).transpose(2, 1, 0, 3).reshape(D, D)
    up = lambda w: w.transpose(1, 0, 2).reshape(D, E * R)
    arrays = {
        "x": a["x"].transpose(1, 2, 0).reshape(T, 2, C // 2, 2, 32).transpose(0, 3, 2, 1, 4),
        "band": band,
        "taps": a["L0_tok_w_temporal"].reshape(C, TAPS).T,
        "wproj": np.concatenate([a["L0_tok_w_proj"].T, a["L0_tok_b_proj"].reshape(1, D)]),
        "gamma": a["L0_tok_ln_gamma"],
        "beta": a["L0_tok_ln_beta"],
        "wqkv": np.concatenate([cols(wqkv[:, :, 1]), cols(wqkv[:, :, 0]), wv], axis=1),
        "wout": a["L0_attn_W_out"].reshape(NH * HD, D),
        "gate": a["L0_ffn_gate_w"],
        "wup": np.concatenate([up(a["L0_ffn_Wu"]), up(a["L0_ffn_Wv"])], axis=1),
        "wdown": a["L0_ffn_Wo"].reshape(E * R, D),
        "constf": constf,
        "constb": constb,
    }
    nc = bacc.Bacc("TRN2", target_bir_lowering=False, num_devices=1)
    feed, args = {}, []
    for name, v in arrays.items():
        v = np.ascontiguousarray(v)
        feed[f"in_{name}"] = v
        args.append(nc.dram_tensor(f"in_{name}", v.shape, mb.dt.from_np(v.dtype), kind="ExternalInput").ap())
    args.append(nc.dram_tensor("out_0", (B, S, D), F32, kind="ExternalOutput").ap())
    args.append(nc.dram_tensor("v_scratch", (NJ, 128, D), F32).ap())
    args.append(nc.dram_tensor("o_scratch", (Q4, 128, D), F32).ap())
    build(nc, *args)
    r = run(nc, [feed], core_ids=[0])
    return r.results[0]["out_0"]
```
